# Optimizing a Trainium2 kernel written in Bass

```python
import numpy as np
import jax
import jax.numpy as jnp

def _softmax(x, axis=-1):
    return jax.nn.softmax(x, axis=axis)

def _gelu(x):
    return jax.nn.gelu(x, approximate=True)

def _silu(x):
    return jax.nn.silu(x)

def _sigmoid(x):
    return jax.nn.sigmoid(x)

def _layernorm(x, axis=-1, eps=1e-05):
    m = jnp.mean(x, axis=axis, keepdims=True)
    v = jnp.var(x, axis=axis, keepdims=True)
    return (x - m) / jnp.sqrt(v + eps)

def _scatter_add(tgt, idx, src, axis=0):
    return tgt.at[idx].add(src)

def _segment_sum(src, seg, n):
    return jax.ops.segment_sum(src, seg, n)
kernel_name = 'mk_gps_d2_gnn_r8_13fd0c'

def setup_inputs(seed: int=0):
    np.random.seed(seed)
    _w = jnp.asarray

    def _rec_inputs():
        import jax
        import jax.numpy as jnp
        _gk = jax.random.key(seed)
        x = -6.415e-05 + 1 * jax.random.normal(jax.random.fold_in(_gk, 1), (1250, 512), jnp.float32)
        _s = jax.random.randint(jax.random.fold_in(_gk, 2), (10000,), 0, 1250, jnp.int32)
        _d = jax.random.randint(jax.random.fold_in(_gk, 3), (10000,), 0, 1250, jnp.int32)
        _loop = jnp.arange(1250, dtype=jnp.int32)
        src = jnp.concatenate([_s, _d, _loop])
        dst = jnp.concatenate([_d, _s, _loop])
        _o = jnp.argsort(dst, stable=True)
        src = src[_o]
        dst = dst[_o]
        edge_attr_8 = 0.000735704 + 1.0001 * jax.random.normal(jax.random.fold_in(_gk, 11), (21250, 8), jnp.float32)
        return (x, src, dst, edge_attr_8)
    x, src, dst, edge_attr_8 = _rec_inputs()

    def _L0_gnn_setup():
        import jax, jax.numpy as jnp
        import numpy as np
        L, E = (2500, 40000)
        C, HID, H = (512, 1024, 8)
        D = C // H
        EPS = 1e-05

        def _layernorm(x, g, b):
            mu = jnp.mean(x, axis=-1, keepdims=True)
            var = jnp.mean(jnp.square(x - mu), axis=-1, keepdims=True)
            return (x - mu) * jax.lax.rsqrt(var + EPS) * g + b
        key = jax.random.key(seed)
        ks = jax.random.split(key, 12)
        s_c = 1.0 / np.sqrt(C)
        s_h = 1.0 / np.sqrt(HID)
        inp = {'x': jax.random.normal(ks[0], (L, C), jnp.float32), 'edge_index': jax.random.randint(ks[1], (2, E), 0, L, jnp.int64), 'att_bias': jax.random.normal(ks[2], (E, H), jnp.float32), 'Wq': jax.random.normal(ks[3], (C, C), jnp.float32) * s_c, 'bq': jnp.zeros((C,), jnp.float32), 'Wk': jax.random.normal(ks[4], (C, C), jnp.float32) * s_c, 'bk': jnp.zeros((C,), jnp.float32), 'Wv': jax.random.normal(ks[5], (C, C), jnp.float32) * s_c, 'bv': jnp.zeros((C,), jnp.float32), 'Wo': jax.random.normal(ks[6], (C, C), jnp.float32) * s_c, 'bo': jnp.zeros((C,), jnp.float32), 'ln_att_g': jnp.ones((C,), jnp.float32), 'ln_att_b': jnp.zeros((C,), jnp.float32), 'ln_ff_g': jnp.ones((C,), jnp.float32), 'ln_ff_b': jnp.zeros((C,), jnp.float32), 'W1': jax.random.normal(ks[7], (HID, C), jnp.float32) * s_c, 'b1': jnp.zeros((HID,), jnp.float32), 'W2': jax.random.normal(ks[8], (C, HID), jnp.float32) * s_h, 'b2': jnp.zeros((C,), jnp.float32)}
        return inp
    _L0_gnn_all = _L0_gnn_setup()
    _L0_gnn_in = {k: v for k, v in _L0_gnn_all.items() if k in ('Wq', 'bq', 'Wk', 'bk', 'Wv', 'bv', 'Wo', 'bo', 'ln_att_g', 'ln_att_b', 'ln_ff_g', 'ln_ff_b', 'W1', 'b1', 'W2', 'b2')}
    del _L0_gnn_all

    def _L0_mix_setup():
        import jax, jax.numpy as jnp
        import numpy as np
        B, N, C = (8, 512, 512)
        key = jax.random.key(seed)
        ks = jax.random.split(key, 6)
        s = 1.0 / np.sqrt(C)
        return {'x': jax.random.normal(ks[0], (B, N, C), jnp.float32), 'Wq': jax.random.normal(ks[1], (C, C), jnp.float32) * s, 'Wk': jax.random.normal(ks[2], (C, C), jnp.float32) * s, 'Wv': jax.random.normal(ks[3], (C, C), jnp.float32) * s, 'W1': jax.random.normal(ks[4], (C, C), jnp.float32) * s, 'W2': jax.random.normal(ks[5], (C, C), jnp.float32) * s}
    _L0_mix_all = _L0_mix_setup()
    _L0_mix_in = {k: v for k, v in _L0_mix_all.items() if k in ('Wq', 'Wk', 'Wv', 'W1', 'W2')}
    del _L0_mix_all

    def _L0_ffn_setup():
        import jax, jax.numpy as jnp
        import numpy as np
        INPUT_SIZE = 512
        HIDDEN_SIZE = 512
        key = jax.random.key(seed)
        ks = jax.random.split(key, 9)
        B, T, I, H = (64, 512, INPUT_SIZE, HIDDEN_SIZE)
        scale = 1.0 / np.sqrt(I + H)
        x = jax.random.normal(ks[0], (B, T, I), dtype=jnp.float32)

        def lin(kw, kb):
            W = jax.random.uniform(kw, (I + H, H), minval=-scale, maxval=scale, dtype=jnp.float32)
            b = jax.random.uniform(kb, (H,), minval=-scale, maxval=scale, dtype=jnp.float32)
            return (W, b)
        W_f, b_f = lin(ks[1], ks[2])
        W_i, b_i = lin(ks[3], ks[4])
        W_c, b_c = lin(ks[5], ks[6])
        W_o, b_o = lin(ks[7], ks[8])
        return {'x': x, 'W_f': W_f, 'b_f': b_f, 'W_i': W_i, 'b_i': b_i, 'W_c': W_c, 'b_c': b_c, 'W_o': W_o, 'b_o': b_o}
    _L0_ffn_all = _L0_ffn_setup()
    _L0_ffn_in = {k: v for k, v in _L0_ffn_all.items() if k in ('W_f', 'b_f', 'W_i', 'b_i', 'W_c', 'b_c', 'W_o', 'b_o')}
    del _L0_ffn_all

    def _L1_gnn_setup():
        import jax, jax.numpy as jnp
        import numpy as np
        N = 6250
        E = 50000
        D_IN = 512
        D_HID = 256
        D_OUT = 512
        key = jax.random.key(seed)
        k1, k2, k3, k4 = jax.random.split(key, 4)
        x = jax.random.normal(k1, (N, D_IN), dtype=jnp.float32)
        edge_index = jax.random.randint(k2, (2, E), 0, N, dtype=jnp.int64)
        W1 = jax.random.normal(k3, (D_IN, D_HID), dtype=jnp.float32) * (1.0 / np.sqrt(D_IN))
        b1 = jnp.zeros((D_HID,), dtype=jnp.float32)
        W2 = jax.random.normal(k4, (D_HID, D_OUT), dtype=jnp.float32) * (1.0 / np.sqrt(D_HID))
        b2 = jnp.zeros((D_OUT,), dtype=jnp.float32)
        return {'x': x, 'edge_index': edge_index, 'W1': W1, 'b1': b1, 'W2': W2, 'b2': b2}
    _L1_gnn_all = _L1_gnn_setup()
    _L1_gnn_in = {k: v for k, v in _L1_gnn_all.items() if k in ('W1', 'b1', 'W2', 'b2')}
    del _L1_gnn_all

    def _L1_mix_setup():
        import jax, jax.numpy as jnp
        import numpy as np
        DIM = 512
        HEADS = 8
        HEAD_DIM = DIM // HEADS
        key = jax.random.key(seed)
        ks = jax.random.split(key, 9)
        B, T, C = (8, 1024, DIM)
        s = 1.0 / np.sqrt(C)
        x = jax.random.normal(ks[0], (B, T, C), dtype=jnp.float32)
        Wq = jax.random.uniform(ks[1], (C, C), jnp.float32, -s, s)
        bq = jax.random.uniform(ks[2], (C,), jnp.float32, -s, s)
        Wk = jax.random.uniform(ks[3], (C, C), jnp.float32, -s, s)
        bk = jax.random.uniform(ks[4], (C,), jnp.float32, -s, s)
        Wv = jax.random.uniform(ks[5], (C, C), jnp.float32, -s, s)
        bv = jax.random.uniform(ks[6], (C,), jnp.float32, -s, s)
        Wo = jax.random.uniform(ks[7], (C, C), jnp.float32, -s, s)
        bo = jax.random.uniform(ks[8], (C,), jnp.float32, -s, s)
        return {'x': x, 'Wq': Wq, 'bq': bq, 'Wk': Wk, 'bk': bk, 'Wv': Wv, 'bv': bv, 'Wo': Wo, 'bo': bo}
    _L1_mix_all = _L1_mix_setup()
    _L1_mix_in = {k: v for k, v in _L1_mix_all.items() if k in ('Wq', 'bq', 'Wk', 'bk', 'Wv', 'bv', 'Wo', 'bo')}
    del _L1_mix_all

    def _L1_ffn_setup():
        import jax, jax.numpy as jnp
        import numpy as np
        D_MODEL = 512
        DFF = 256
        TOP_K = 2
        EXPERTS_PER_LEVEL = (4, 8)

        def _moe_level(x, Wr, W1, b1, W2, b2, k):
            probs = jax.nn.softmax(jnp.einsum('bsd,de->bse', x, Wr), axis=-1)
            _, top_idx = jax.lax.top_k(probs, k)
            dispatch = jax.nn.one_hot(top_idx, probs.shape[-1], dtype=x.dtype).sum(axis=-2)
            xm = x[:, :, None, :] * dispatch[..., None]
            h = jax.nn.relu(jnp.einsum('bsed,edf->bsef', xm, W1) + b1)
            y = jnp.einsum('bsef,efd->bsed', h, W2) + b2
            return jnp.sum(y * probs[..., None], axis=2)
        key = jax.random.key(seed)
        ks = jax.random.split(key, 12)

        def w(k, fan_in, shape):
            return jax.random.normal(k, shape, jnp.float32) * (1.0 / np.sqrt(fan_in))

        def b(k, shape):
            return jax.random.normal(k, shape, jnp.float32) * 0.01
        E0, E1 = EXPERTS_PER_LEVEL
        return {'x': jax.random.normal(ks[0], (4, 256, D_MODEL), jnp.float32), 'Wr0': w(ks[1], D_MODEL, (D_MODEL, E0)), 'W1_0': w(ks[2], D_MODEL, (E0, D_MODEL, DFF)), 'b1_0': b(ks[3], (E0, DFF)), 'W2_0': w(ks[4], DFF, (E0, DFF, D_MODEL)), 'b2_0': b(ks[5], (E0, D_MODEL)), 'Wr1': w(ks[6], D_MODEL, (D_MODEL, E1)), 'W1_1': w(ks[7], D_MODEL, (E1, D_MODEL, DFF)), 'b1_1': b(ks[8], (E1, DFF)), 'W2_1': w(ks[9], DFF, (E1, DFF, D_MODEL)), 'b2_1': b(ks[10], (E1, D_MODEL))}
    _L1_ffn_all = _L1_ffn_setup()
    _L1_ffn_in = {k: v for k, v in _L1_ffn_all.items() if k in ('Wr0', 'W1_0', 'b1_0', 'W2_0', 'b2_0', 'Wr1', 'W1_1', 'b1_1', 'W2_1', 'b2_1')}
    del _L1_ffn_all
    return {'x': x, 'src': src, 'dst': dst, 'edge_attr_8': edge_attr_8, 'L0_gnn_Wq': _L0_gnn_in['Wq'], 'L0_gnn_bq': _L0_gnn_in['bq'], 'L0_gnn_Wk': _L0_gnn_in['Wk'], 'L0_gnn_bk': _L0_gnn_in['bk'], 'L0_gnn_Wv': _L0_gnn_in['Wv'], 'L0_gnn_bv': _L0_gnn_in['bv'], 'L0_gnn_Wo': _L0_gnn_in['Wo'], 'L0_gnn_bo': _L0_gnn_in['bo'], 'L0_gnn_ln_att_g': _L0_gnn_in['ln_att_g'], 'L0_gnn_ln_att_b': _L0_gnn_in['ln_att_b'], 'L0_gnn_ln_ff_g': _L0_gnn_in['ln_ff_g'], 'L0_gnn_ln_ff_b': _L0_gnn_in['ln_ff_b'], 'L0_gnn_W1': _L0_gnn_in['W1'], 'L0_gnn_b1': _L0_gnn_in['b1'], 'L0_gnn_W2': _L0_gnn_in['W2'], 'L0_gnn_b2': _L0_gnn_in['b2'], 'L0_mix_Wq': _L0_mix_in['Wq'], 'L0_mix_Wk': _L0_mix_in['Wk'], 'L0_mix_Wv': _L0_mix_in['Wv'], 'L0_mix_W1': _L0_mix_in['W1'], 'L0_mix_W2': _L0_mix_in['W2'], 'L0_ffn_W_f': _L0_ffn_in['W_f'], 'L0_ffn_b_f': _L0_ffn_in['b_f'], 'L0_ffn_W_i': _L0_ffn_in['W_i'], 'L0_ffn_b_i': _L0_ffn_in['b_i'], 'L0_ffn_W_c': _L0_ffn_in['W_c'], 'L0_ffn_b_c': _L0_ffn_in['b_c'], 'L0_ffn_W_o': _L0_ffn_in['W_o'], 'L0_ffn_b_o': _L0_ffn_in['b_o'], 'L1_gnn_W1': _L1_gnn_in['W1'], 'L1_gnn_b1': _L1_gnn_in['b1'], 'L1_gnn_W2': _L1_gnn_in['W2'], 'L1_gnn_b2': _L1_gnn_in['b2'], 'L1_mix_Wq': _L1_mix_in['Wq'], 'L1_mix_bq': _L1_mix_in['bq'], 'L1_mix_Wk': _L1_mix_in['Wk'], 'L1_mix_bk': _L1_mix_in['bk'], 'L1_mix_Wv': _L1_mix_in['Wv'], 'L1_mix_bv': _L1_mix_in['bv'], 'L1_mix_Wo': _L1_mix_in['Wo'], 'L1_mix_bo': _L1_mix_in['bo'], 'L1_ffn_Wr0': _L1_ffn_in['Wr0'], 'L1_ffn_W1_0': _L1_ffn_in['W1_0'], 'L1_ffn_b1_0': _L1_ffn_in['b1_0'], 'L1_ffn_W2_0': _L1_ffn_in['W2_0'], 'L1_ffn_b2_0': _L1_ffn_in['b2_0'], 'L1_ffn_Wr1': _L1_ffn_in['Wr1'], 'L1_ffn_W1_1': _L1_ffn_in['W1_1'], 'L1_ffn_b1_1': _L1_ffn_in['b1_1'], 'L1_ffn_W2_1': _L1_ffn_in['W2_1'], 'L1_ffn_b2_1': _L1_ffn_in['b2_1']}

def reference(x, src, dst, edge_attr_8, L0_gnn_Wq, L0_gnn_bq, L0_gnn_Wk, L0_gnn_bk, L0_gnn_Wv, L0_gnn_bv, L0_gnn_Wo, L0_gnn_bo, L0_gnn_ln_att_g, L0_gnn_ln_att_b, L0_gnn_ln_ff_g, L0_gnn_ln_ff_b, L0_gnn_W1, L0_gnn_b1, L0_gnn_W2, L0_gnn_b2, L0_mix_Wq, L0_mix_Wk, L0_mix_Wv, L0_mix_W1, L0_mix_W2, L0_ffn_W_f, L0_ffn_b_f, L0_ffn_W_i, L0_ffn_b_i, L0_ffn_W_c, L0_ffn_b_c, L0_ffn_W_o, L0_ffn_b_o, L1_gnn_W1, L1_gnn_b1, L1_gnn_W2, L1_gnn_b2, L1_mix_Wq, L1_mix_bq, L1_mix_Wk, L1_mix_bk, L1_mix_Wv, L1_mix_bv, L1_mix_Wo, L1_mix_bo, L1_ffn_Wr0, L1_ffn_W1_0, L1_ffn_b1_0, L1_ffn_W2_0, L1_ffn_b2_0, L1_ffn_Wr1, L1_ffn_W1_1, L1_ffn_b1_1, L1_ffn_W2_1, L1_ffn_b2_1):
    import jax
    import jax.numpy as jnp

    def _L0_gnn_ref(x, edge_index, att_bias, Wq, bq, Wk, bk, Wv, bv, Wo, bo, ln_att_g, ln_att_b, ln_ff_g, ln_ff_b, W1, b1, W2, b2):
        import jax, jax.numpy as jnp
        import numpy as np
        L, E = (2500, 40000)
        C, HID, H = (512, 1024, 8)
        D = C // H
        EPS = 1e-05

        def _layernorm(x, g, b):
            mu = jnp.mean(x, axis=-1, keepdims=True)
            var = jnp.mean(jnp.square(x - mu), axis=-1, keepdims=True)
            return (x - mu) * jax.lax.rsqrt(var + EPS) * g + b
        n = x.shape[0]
        src = edge_index[0]
        dst = edge_index[1]
        z = _layernorm(x, ln_att_g, ln_att_b)
        q = (z @ Wq.T + bq).reshape(n, H, D)
        k = (z @ Wk.T + bk).reshape(n, H, D)
        v = (z @ Wv.T + bv).reshape(n, H, D)
        s = jnp.einsum('ehd,ehd->eh', q[src], k[dst]) / np.sqrt(D) + att_bias
        m = jax.ops.segment_max(s, src, num_segments=n)
        p = jnp.exp(s - m[src])
        denom = jax.ops.segment_sum(p, src, num_segments=n)
        alpha = p / jnp.where(denom[src] == 0, 1.0, denom[src])
        agg = jax.ops.segment_sum(alpha[:, :, None] * v[dst], src, num_segments=n)
        att = agg.reshape(n, C) @ Wo.T + bo
        x = x + att
        z = _layernorm(x, ln_ff_g, ln_ff_b)
        h = jax.nn.silu(z @ W1.T + b1)
        ff = h @ W2.T + b2
        return x + ff

    def _L0_mix_ref(x, Wq, Wk, Wv, W1, W2):
        import jax, jax.numpy as jnp
        import numpy as np
        B, N, C = (8, 512, 512)
        q = x @ Wq.T
        k = x @ Wk.T
        v = x @ Wv.T
        dim = q.shape[-1]
        q = jax.nn.softmax(q, axis=-1) * dim ** (-0.5)
        k = jax.nn.softmax(k, axis=-2)
        context = jnp.einsum('bnd,bne->bde', k, v)
        attn = jnp.einsum('bnd,bde->bne', q, context)
        x = attn + x
        return x @ W1.T @ W2.T + x

    def _L0_ffn_ref(x, W_f, b_f, W_i, b_i, W_c, b_c, W_o, b_o):
        import jax, jax.numpy as jnp
        import numpy as np
        INPUT_SIZE = 512
        HIDDEN_SIZE = 512
        B, T, I = x.shape
        H = W_f.shape[1]
        h0 = jnp.zeros((B, H), dtype=x.dtype)
        c0 = jnp.zeros((B, H), dtype=x.dtype)

        def step(carry, x_t):
            h_prev, c_prev = carry
            combined = jnp.concatenate((x_t, h_prev), axis=1)
            f_t = jax.nn.sigmoid(combined @ W_f + b_f)
            i_t = jax.nn.sigmoid(combined @ W_i + b_i)
            c_tilde = jnp.tanh(combined @ W_c + b_c)
            c_t = f_t * c_prev + i_t * c_tilde
            o_t = jax.nn.sigmoid(combined @ W_o + b_o)
            h_t = o_t * jnp.tanh(c_t)
            return ((h_t, c_t), h_t)
        _, hs = jax.lax.scan(step, (h0, c0), jnp.swapaxes(x, 0, 1))
        return jnp.swapaxes(hs, 0, 1)

    def _L1_gnn_ref(x, edge_index, W1, b1, W2, b2):
        import jax, jax.numpy as jnp
        import numpy as np
        N = 6250
        E = 50000
        D_IN = 512
        D_HID = 256
        D_OUT = 512
        h = jax.nn.relu(x @ W1 + b1) @ W2 + b2
        row, col = (edge_index[0], edge_index[1])
        agg = jax.ops.segment_sum(h[col], row, num_segments=h.shape[0])
        return h + agg

    def _L1_mix_ref(x, Wq, bq, Wk, bk, Wv, bv, Wo, bo):
        import jax, jax.numpy as jnp
        import numpy as np
        DIM = 512
        HEADS = 8
        HEAD_DIM = DIM // HEADS
        B, T, C = x.shape
        H, D = (HEADS, HEAD_DIM)

        def proj(W, b):
            return (x @ W.T + b).reshape(B, T, H, D).transpose(0, 2, 1, 3)
        Q = proj(Wq, bq)
        K = proj(Wk, bk)
        V = proj(Wv, bv)
        Q = jax.nn.elu(Q) + 1.0
        K = jax.nn.elu(K) + 1.0
        KV = jnp.einsum('bhnd,bhne->bhde', K, V)
        Q_KV = jnp.einsum('bhnd,bhde->bhne', Q, KV)
        K_sum = K.sum(axis=2)
        normalizer = jnp.einsum('bhnd,bhd->bhn', Q, K_sum)
        out = Q_KV / (normalizer[..., None] + 1e-06)
        out = out.transpose(0, 2, 1, 3).reshape(B, T, C)
        out = out @ Wo.T + bo
        return out

    def _L1_ffn_ref(x, Wr0, W1_0, b1_0, W2_0, b2_0, Wr1, W1_1, b1_1, W2_1, b2_1):
        import jax, jax.numpy as jnp
        import numpy as np
        D_MODEL = 512
        DFF = 256
        TOP_K = 2
        EXPERTS_PER_LEVEL = (4, 8)

        def _moe_level(x, Wr, W1, b1, W2, b2, k):
            probs = jax.nn.softmax(jnp.einsum('bsd,de->bse', x, Wr), axis=-1)
            _, top_idx = jax.lax.top_k(probs, k)
            dispatch = jax.nn.one_hot(top_idx, probs.shape[-1], dtype=x.dtype).sum(axis=-2)
            xm = x[:, :, None, :] * dispatch[..., None]
            h = jax.nn.relu(jnp.einsum('bsed,edf->bsef', xm, W1) + b1)
            y = jnp.einsum('bsef,efd->bsed', h, W2) + b2
            return jnp.sum(y * probs[..., None], axis=2)
        h0 = _moe_level(x, Wr0, W1_0, b1_0, W2_0, b2_0, TOP_K)
        out = _moe_level(h0, Wr1, W1_1, b1_1, W2_1, b2_1, TOP_K)
        return out
    edge_index = jnp.stack([src, dst])
    xn = _layernorm(x, axis=-1)
    x = x + _L0_gnn_ref(xn, edge_index, edge_attr_8, L0_gnn_Wq, L0_gnn_bq, L0_gnn_Wk, L0_gnn_bk, L0_gnn_Wv, L0_gnn_bv, L0_gnn_Wo, L0_gnn_bo, L0_gnn_ln_att_g, L0_gnn_ln_att_b, L0_gnn_ln_ff_g, L0_gnn_ln_ff_b, L0_gnn_W1, L0_gnn_b1, L0_gnn_W2, L0_gnn_b2) + _L0_mix_ref(xn[None], L0_mix_Wq, L0_mix_Wk, L0_mix_Wv, L0_mix_W1, L0_mix_W2)[0]
    x = x + _L0_ffn_ref(_layernorm(x, axis=-1)[None], L0_ffn_W_f, L0_ffn_b_f, L0_ffn_W_i, L0_ffn_b_i, L0_ffn_W_c, L0_ffn_b_c, L0_ffn_W_o, L0_ffn_b_o)[0]
    xn = _layernorm(x, axis=-1)
    x = x + _L1_gnn_ref(xn, edge_index, L1_gnn_W1, L1_gnn_b1, L1_gnn_W2, L1_gnn_b2) + _L1_mix_ref(xn[None], L1_mix_Wq, L1_mix_bq, L1_mix_Wk, L1_mix_bk, L1_mix_Wv, L1_mix_bv, L1_mix_Wo, L1_mix_bo)[0]
    x = x + _L1_ffn_ref(_layernorm(x, axis=-1)[None], L1_ffn_Wr0, L1_ffn_W1_0, L1_ffn_b1_0, L1_ffn_W2_0, L1_ffn_b2_0, L1_ffn_Wr1, L1_ffn_W1_1, L1_ffn_b1_1, L1_ffn_W2_1, L1_ffn_b2_1)[0]
    return x

_drawn_inputs = setup_inputs


def setup_inputs(seed=0):
    import zlib

    import numpy as np

    out = dict(_drawn_inputs(seed))
    spreads = {'L0_gnn_bq': (0.0, 0.8),
     'L0_gnn_bk': (0.0, 2.0),
     'L0_gnn_bv': (0.0, 0.1),
     'L0_gnn_bo': (0.0, 0.1),
     'L0_gnn_ln_att_g': (1.0, 0.6),
     'L0_gnn_ln_att_b': (0.0, 0.1),
     'L0_gnn_ln_ff_g': (1.0, 0.6),
     'L0_gnn_ln_ff_b': (0.0, 0.401),
     'L0_gnn_b1': (0.0, 0.414),
     'L0_gnn_b2': (0.0, 0.1),
     'L1_gnn_b1': (0.0, 0.1),
     'L1_gnn_b2': (0.0, 0.1)}
    factors = {'L0_mix_Wq': 8.0,
     'L0_mix_Wk': 8.0,
     'L0_mix_Wv': 8.0,
     'L0_ffn_W_f': 8.0,
     'L0_ffn_b_f': 25.534,
     'L0_ffn_W_i': 8.0,
     'L0_ffn_b_i': 24.75,
     'L0_ffn_W_c': 3.111,
     'L0_ffn_b_c': 8.0,
     'L0_ffn_W_o': 8.0,
     'L0_ffn_b_o': 8.0,
     'L1_mix_Wq': 8.0,
     'L1_mix_bq': 34.347,
     'L1_mix_Wk': 8.0,
     'L1_mix_bk': 37.247,
     'L1_mix_Wv': 8.0,
     'L1_mix_bv': 8.0,
     'L1_mix_Wo': 8.0,
     'L1_mix_bo': 8.0,
     'L1_ffn_Wr0': 8.0,
     'L1_ffn_W1_0': 5.342,
     'L1_ffn_b1_0': 8.0,
     'L1_ffn_W2_0': 5.256,
     'L1_ffn_b2_0': 8.0,
     'L1_ffn_Wr1': 6.697,
     'L1_ffn_W1_1': 6.715,
     'L1_ffn_b1_1': 64.0,
     'L1_ffn_W2_1': 5.514,
     'L1_ffn_b2_1': 64.0}
    for name, (base, spread) in spreads.items():
        noise = np.random.default_rng([zlib.crc32(name.encode()), seed]).standard_normal(out[name].shape)
        drawn = base * np.exp(spread * noise) if base else spread * noise
        out[name] = jnp.asarray(drawn.astype(out[name].dtype))
    for name, factor in factors.items():
        out[name] = (out[name] * factor).astype(out[name].dtype)
    return out
```

```python
from contextlib import ExitStack, contextmanager

import numpy as np

import concourse.bass as bass
from concourse import mybir

F32 = mybir.dt.float32
F16 = mybir.dt.float16
BF16 = mybir.dt.bfloat16
I32 = mybir.dt.int32
ALU = mybir.AluOpType
ACT = mybir.ActivationFunctionType
AX = mybir.AxisListType
RMAX = bass.bass_isa.ReduceOp.max

P = 128
N = 1250
E = 21250
C = 512
KC = C // P
RT = -(-N // P)
NP = RT * P
LAST = N - (RT - 1) * P
COLS = [(a, min(512, NP - a)) for a in range(0, NP, 512)]
H, D = 8, 64
HID = 1024
ET = -(-E // P)
EP = ET * P
ST = (EP + RT * (P - 1)) // P
FIELDS = 3 + H
BIG = 1.0e38
EPS = 1e-5


class Ctx:

    def __init__(self, nc):
        self.nc = nc
        self.chained = 0
        self.used = []

    @contextmanager
    def semaphore(self, name):
        handle = self.nc.alloc_semaphore(name=name)
        self.used.append(handle)
        yield handle

    def end_phase(self):
        self.nc.all_engine_barrier()
        self.nc.clear_and_free_semaphores(self.used)
        self.nc.all_engine_barrier()
        self.used = []

    def link(self, eng, ins):
        self.chained += 1
        ins.then_inc(self.dve_chain, 1)
        eng.wait_ge(self.dve_chain, self.chained)


def feature_major(ap, k=KC):
    return ap.rearrange("p (k n) -> p k n", k=k)


def products(g, name, groups, evacuate, by="vector", loads=(), ring=4):
    nc = g.nc
    with ExitStack() as ctx:
        banks = [ctx.enter_context(nc.psum_tensor(f"{name}_bank{i}", [P, 512], F32)) for i in range(ring)]
        summed = ctx.enter_context(g.semaphore(f"{name}_summed"))
        emptied = ctx.enter_context(g.semaphore(f"{name}_emptied"))
        loaded = ctx.enter_context(g.semaphore(f"{name}_loaded"))
        block = ctx.enter_context(nc.Block())

        @block.tensor
        def _(pe):
            for n, terms in enumerate(groups):
                if n >= ring:
                    pe.wait_ge(emptied, n - ring + 1)
                rows, cols = terms[0][0].shape[-1], terms[0][1].shape[-1]
                for i, (lhsT, rhs) in enumerate(terms):
                    mm = pe.matmul(banks[n % ring][0:rows, 0:cols], lhsT, rhs,
                                   start=(i == 0), stop=(i == len(terms) - 1))
                mm.then_inc(summed, 1)

        def empty(eng):
            for n, terms in enumerate(groups):
                eng.wait_ge(summed, n + 1)
                rows, cols = terms[0][0].shape[-1], terms[0][1].shape[-1]
                evacuate(eng, n, banks[n % ring][0:rows, 0:cols]).then_inc(emptied, 1)

        if by == "vector":
            @block.vector
            def _(dve):
                empty(dve)
        else:
            @block.scalar
            def _(act):
                empty(act)

        if loads:
            @block.sync
            def _(sp):
                for dst, src in loads:
                    sp.dma_start(dst, src).then_inc(loaded, 16)
                sp.wait_ge(loaded, 16 * len(loads))


def transfer(g, name, pairs):
    nc = g.nc
    with g.semaphore(f"{name}_moved") as moved, nc.Block() as block:
        @block.sync
        def _(sp):
            for dst, src in pairs:
                sp.dma_start(dst, src).then_inc(moved, 16)
            sp.wait_ge(moved, 16 * len(pairs))


def on_vector(g, steps):
    with g.nc.Block(no_gpsimd_drain=True) as block:
        @block.vector
        def _(dve):
            for make in steps:
                g.link(dve, make(dve))


def on_scalar(g, name, steps):
    with g.nc.Block(no_gpsimd_drain=True) as block:
        @block.scalar
        def _(act):
            for make in steps:
                make(act)


def transposes(g, name, blocks, dst_of, dtype=F32, per_bank=4, by="vector"):
    nc = g.nc
    ident = g.ident if dtype == F32 else g.ident_bf
    m = blocks[0].shape[-1]
    batches = [blocks[i:i + per_bank] for i in range(0, len(blocks), per_bank)]
    with ExitStack() as ctx:
        banks = [ctx.enter_context(nc.psum_tensor(f"{name}_bank{i}", [P, per_bank, P], dtype)) for i in range(3)]
        turned = ctx.enter_context(g.semaphore(f"{name}_turned"))
        copied = ctx.enter_context(g.semaphore(f"{name}_copied"))
        block = ctx.enter_context(nc.Block(no_gpsimd_drain=True))

        @block.tensor
        def _(pe):
            for j, batch in enumerate(batches):
                if j >= 3:
                    pe.wait_ge(copied, j - 2)
                for i, src in enumerate(batch):
                    last = pe.transpose(banks[j % 3][0:m, i, :], src, ident[:, :])
                last.then_inc(turned, 1)

        def copy_out(eng):
            for j, batch in enumerate(batches):
                eng.wait_ge(turned, j + 1)
                src = banks[j % 3][0:m, 0:len(batch), :]
                if by == "vector":
                    ins = eng.tensor_copy(dst_of(j, len(batch)), src)
                else:
                    ins = eng.activation(dst_of(j, len(batch)), src, ACT.Copy)
                ins.then_inc(copied, 1)

        if by == "vector":
            @block.vector
            def _(dve):
                copy_out(dve)
        else:
            @block.scalar
            def _(act):
                copy_out(act)


def constants(g):
    nc = g.nc
    with g.semaphore("filled") as filled, g.semaphore("cut") as cut, nc.Block() as block:
        @block.gpsimd
        def _(pool):
            pool.memset(g.ident[:, :], 0.0).then_inc(filled, 1)
            pool.memset(g.below[:, :], 1.0).then_inc(filled, 1)
            pool.memset(g.above[:, :], 1.0).then_inc(filled, 1)
            pool.memset(g.mean[:, :], 1.0 / C).then_inc(filled, 1)
            pool.memset(g.ones[:, :], 1.0).then_inc(filled, 1)
            pool.iota(g.numbers[:, :], pattern=[[1, P]], base=0, channel_multiplier=0).then_inc(filled, 1)
            pool.memset(g.sel[:, :, :], 0.0).then_inc(filled, 1)
            pool.wait_ge(filled, 7)
            pool.affine_select(out=g.ident[:, :], in_=g.ident[:, :], compare_op=ALU.not_equal, fill=1.0,
                               base=0, pattern=[[-1, P]], channel_multiplier=1).then_inc(cut, 1)
            pool.affine_select(out=g.below[:, :], in_=g.below[:, :], compare_op=ALU.is_gt, fill=0.0,
                               base=0, pattern=[[1, P]], channel_multiplier=-1).then_inc(cut, 1)
            pool.affine_select(out=g.above[:, :], in_=g.above[:, :], compare_op=ALU.is_gt, fill=0.0,
                               base=0, pattern=[[-1, P]], channel_multiplier=1).then_inc(cut, 1)
            pool.affine_select(out=g.sel[:, :, :], in_=g.sel[:, :, :], compare_op=ALU.not_equal, fill=1.0,
                               base=0, pattern=[[-1, 8], [0, P]], channel_multiplier=1).then_inc(cut, 1)

        @block.vector
        def _(dve):
            dve.wait_ge(cut, 4)
            dve.tensor_copy(g.ident_bf[:, :], g.ident[:, :])
            dve.tensor_copy(g.numbers_f[:, :], g.numbers[:, :])


def layer_norm(g, name, src, dst, gain=None, shift=None, loads=(), sq=None):
    nc = g.nc
    with ExitStack() as ctx:
        mean = [ctx.enter_context(nc.psum_tensor(f"{name}_mean{c}", [P, 512], F32)) for c in range(len(COLS))]
        var = [ctx.enter_context(nc.psum_tensor(f"{name}_var{c}", [P, 512], F32)) for c in range(len(COLS))]
        if sq is None:
            sq = ctx.enter_context(nc.sbuf_tensor(f"{name}_sq", [P, KC, NP], F32))
        rstd = ctx.enter_context(nc.sbuf_tensor(f"{name}_rstd", [P, NP], F32))
        s_mean = ctx.enter_context(g.semaphore(f"{name}_s_mean"))
        s_centred = ctx.enter_context(g.semaphore(f"{name}_s_centred"))
        s_squared = ctx.enter_context(g.semaphore(f"{name}_s_squared"))
        s_var = ctx.enter_context(g.semaphore(f"{name}_s_var"))
        s_eps = ctx.enter_context(g.semaphore(f"{name}_s_eps"))
        s_root = ctx.enter_context(g.semaphore(f"{name}_s_root"))
        s_rstd = ctx.enter_context(g.semaphore(f"{name}_s_rstd"))
        s_scaled = ctx.enter_context(g.semaphore(f"{name}_s_scaled"))
        loaded = ctx.enter_context(g.semaphore(f"{name}_loaded"))
        block = ctx.enter_context(nc.Block())

        @block.tensor
        def _(pe):
            for c, (a, w) in enumerate(COLS):
                for k in range(KC):
                    mm = pe.matmul(mean[c][:, 0:w], g.mean[:, :], src[:, k, a:a + w],
                                   start=(k == 0), stop=(k == KC - 1))
                mm.then_inc(s_mean, 1)
            for c, (a, w) in enumerate(COLS):
                pe.wait_ge(s_squared, c + 1)
                for k in range(KC):
                    mm = pe.matmul(var[c][:, 0:w], g.mean[:, :], sq[:, k, a:a + w],
                                   start=(k == 0), stop=(k == KC - 1))
                mm.then_inc(s_var, 1)

        @block.vector
        def _(dve):
            for c, (a, w) in enumerate(COLS):
                dve.wait_ge(s_mean, c + 1)
                dve.tensor_tensor(dst[:, :, a:a + w], src[:, :, a:a + w],
                                  mean[c][:, 0:w].unsqueeze(1).broadcast_to([P, KC, w]),
                                  ALU.subtract).then_inc(s_centred, 1)
            for c, (a, w) in enumerate(COLS):
                dve.wait_ge(s_var, c + 1)
                dve.tensor_scalar(rstd[:, a:a + w], var[c][:, 0:w], EPS, None, ALU.add).then_inc(s_eps, 1)
            for c, (a, w) in enumerate(COLS):
                dve.wait_ge(s_root, c + 1)
                dve.reciprocal(rstd[:, a:a + w], rstd[:, a:a + w]).then_inc(s_rstd, 1)
                dve.wait_ge(s_rstd, c + 1)
                dve.tensor_tensor(dst[:, :, a:a + w], dst[:, :, a:a + w],
                                  rstd[:, a:a + w].unsqueeze(1).broadcast_to([P, KC, w]),
                                  ALU.mult).then_inc(s_scaled, 1)

        @block.scalar
        def _(act):
            for c, (a, w) in enumerate(COLS):
                act.wait_ge(s_centred, c + 1)
                act.activation(sq[:, :, a:a + w], dst[:, :, a:a + w], ACT.Square).then_inc(s_squared, 1)
            for c, (a, w) in enumerate(COLS):
                act.wait_ge(s_eps, c + 1)
                act.activation(rstd[:, a:a + w], rstd[:, a:a + w], ACT.Sqrt).then_inc(s_root, 1)
            if gain is not None:
                act.wait_ge(s_scaled, len(COLS))
                for k in range(KC):
                    act.activation(dst[:, k, :], dst[:, k, :], ACT.Identity, scale=gain[:, k:k + 1],
                                   bias=shift[:, k:k + 1])

        if loads:
            @block.sync
            def _(sp):
                for d, s in loads:
                    sp.dma_start(d, s).then_inc(loaded, 16)
                sp.wait_ge(loaded, 16 * len(loads))


def linear(w, x, width=C, chunks=KC):
    return [[(w[:, k, m * P:(m + 1) * P], x[:, k, a:a + n]) for k in range(chunks)]
            for m in range(width // P) for a, n in COLS]


def rows_of(w, x):
    return [[(x[:, k, r * P:(r + 1) * P], w[:, k, :]) for k in range(KC)] for r in range(RT)]


def where(n):
    m, c = divmod(n, len(COLS))
    return m, slice(COLS[c][0], COLS[c][0] + COLS[c][1])


def tables(g, name, x, weights, biases, outs, relu=False, loads=()):
    nc = g.nc
    width = weights[0].shape[-1]
    jobs = [(i, r) for i in range(len(weights)) for r in range(RT)]
    with ExitStack() as ctx:
        bank = [ctx.enter_context(nc.psum_tensor(f"{name}_bank{i}", [P, 512], F32)) for i in range(4)]
        row = ctx.enter_context(nc.sbuf_tensor(f"{name}_row", [P, 4, width], F32))
        summed = ctx.enter_context(g.semaphore(f"{name}_summed"))
        emptied = ctx.enter_context(g.semaphore(f"{name}_emptied"))
        stored = [ctx.enter_context(g.semaphore(f"{name}_stored{i}")) for i in range(4)]
        loaded = ctx.enter_context(g.semaphore(f"{name}_loaded"))
        block = ctx.enter_context(nc.Block())

        @block.tensor
        def _(pe):
            for n, (i, r) in enumerate(jobs):
                if n >= 4:
                    pe.wait_ge(emptied, n - 3)
                for k in range(KC):
                    mm = pe.matmul(bank[n % 4][:, 0:width], x[:, k, r * P:(r + 1) * P], weights[i][:, k, :],
                                   start=(k == 0), stop=(k == KC - 1))
                mm.then_inc(summed, 1)

        @block.vector
        def _(dve):
            for n, (i, r) in enumerate(jobs):
                dve.wait_ge(summed, n + 1)
                if n >= 4:
                    dve.wait_ge(stored[n % 4], 16 * (n // 4))
                ins = dve.tensor_tensor(row[:, n % 4, :], bank[n % 4][:, 0:width], biases[i], ALU.add)
                if relu:
                    g.link(dve, ins)
                    ins = dve.tensor_scalar(row[:, n % 4, :], row[:, n % 4, :], 0.0, None, ALU.max)
                ins.then_inc(emptied, 1)

        @block.sync
        def _(sp):
            for dst, src in loads:
                sp.dma_start(dst, src).then_inc(loaded, 16)
            for n, (i, r) in enumerate(jobs):
                sp.wait_ge(emptied, n + 1)
                sp.dma_start(outs[i][r * P:(r + 1) * P, :], row[:, n % 4, :]).then_inc(stored[n % 4], 16)
            for s in range(4):
                sp.wait_ge(stored[s], 16 * len(range(s, len(jobs), 4)))
            if loads:
                sp.wait_ge(loaded, 16 * len(loads))


def sort_edges(g, src_d, dst_d, attr_d, src_by_tile_d, table, tile_node):
    nc = g.nc
    with ExitStack() as ctx:
        def sb(name, shape, dt=F32):
            return ctx.enter_context(nc.sbuf_tensor(name, shape, dt))

        src_i = sb("src_i", [P, ET], I32)
        part_i = sb("part_i", [P, 2, ET], I32)
        lo = sb("lo", [P, ET])
        hi = sb("hi", [P, ET])
        src_f = sb("src_f", [P, ET])
        edge = sb("edge", [P, ET, FIELDS])
        attr = sb("attr", [P, ET, H])
        dst_i = sb("dst_i", [P, ET], I32)
        is_lo = sb("is_lo", [P, ET, P], BF16)
        is_lo_t = sb("is_lo_t", [P, ET, P], BF16)
        is_hi = sb("is_hi", [P, ET, RT])
        is_hi_bf = sb("is_hi_bf", [P, ET, RT], BF16)
        count = sb("count", [P, RT, ET])
        run = sb("run", [P, RT, ET])
        zeros = sb("zeros", [P, RT * ET])
        total = sb("total", [P, RT])
        node_tot = sb("node_tot", [P, RT])
        tiles_i = sb("tiles_i", [P, RT], I32)
        tiles = sb("tiles", [P, RT])
        tiles_end = sb("tiles_end", [P, RT])
        first_tile = sb("first_tile", [P, RT])
        base = sb("base", [P, RT])
        before = sb("before", [P, RT])
        start_i = sb("start_i", [P, 2, RT * ET], I32)
        start = sb("start", [P, ET, 2, RT], BF16)
        picked = sb("picked", [P, ET, 2, RT])
        digits = sb("digits", [P, ET, 2])
        rank = sb("rank", [P, ET])
        same = sb("same", [P, P])
        pos = sb("pos", [P, ET])
        pos_i = sb("pos_i", [P, ET], I32)
        KT = 21
        keys = sb("keys", [P, 2, KT * P], I32)
        blank = sb("blank", [P, ST, FIELDS])

        with g.semaphore("edges_in") as edges_in, nc.Block() as block:
            @block.sync
            def _(sp):
                sp.dma_start(src_i[:, :], src_d).then_inc(edges_in, 16)
                sp.dma_start(dst_i[:, :], dst_d).then_inc(edges_in, 16)
                sp.dma_start(attr[:, :, :], attr_d).then_inc(edges_in, 16)

            @block.vector
            def _(dve):
                dve.wait_ge(edges_in, 48)
                g.link(dve, dve.tensor_scalar(part_i[:, 0, :], src_i[:, :], P - 1, None, ALU.bitwise_and))
                g.link(dve, dve.tensor_scalar(part_i[:, 1, :], src_i[:, :], 7, None, ALU.logical_shift_right))
                g.link(dve, dve.tensor_copy(lo[:, :], part_i[:, 0, :]))
                g.link(dve, dve.tensor_copy(hi[:, :], part_i[:, 1, :]))
                dve.tensor_copy(src_f[:, :], src_i[:, :])
                dve.tensor_copy(edge[:, :, 0], lo[:, :])
                dve.tensor_copy(edge[:, :, 1].bitcast(I32), src_i[:, :])
                dve.tensor_copy(edge[:, :, 2].bitcast(I32), dst_i[:, :])
                dve.tensor_copy(edge[:, :, 3:3 + H], attr[:, :, :])
                dve.tensor_tensor(is_lo[:, :, :], lo[:, :].unsqueeze(2).broadcast_to([P, ET, P]),
                                  g.numbers_f[:, :].unsqueeze(1).broadcast_to([P, ET, P]), ALU.is_equal)
                g.link(dve, dve.tensor_tensor(is_hi[:, :, :], hi[:, :].unsqueeze(2).broadcast_to([P, ET, RT]),
                                              g.numbers_f[:, 0:RT].unsqueeze(1).broadcast_to([P, ET, RT]),
                                              ALU.is_equal))
                dve.tensor_copy(is_hi_bf[:, :, :], is_hi[:, :, :])
                dve.memset(zeros[:, :], 0.0)

            @block.gpsimd
            def _(pool):
                pool.memset(blank[:, :, 0:1], 255.0)
                pool.memset(blank[:, :, 1:2].bitcast(I32), NP - 1)
                pool.memset(blank[:, :, 2:], 0.0)

        per_bank = 48
        banks_n = -(-ET // per_bank)
        with ExitStack() as inner:
            bank = [inner.enter_context(nc.psum_tensor(f"count_bank{i}", [P, 512], F32)) for i in range(banks_n)]
            blanked = inner.enter_context(g.semaphore("blanked"))
            counted = inner.enter_context(g.semaphore("counted"))
            block = inner.enter_context(nc.Block())

            @block.sync
            def _(sp):
                sp.dma_start(table.rearrange("(p t) f -> p (t f)", p=P),
                             blank[:, :, :].rearrange("p t f -> p (t f)")).then_inc(blanked, 16)
                sp.wait_ge(blanked, 16)

            @block.tensor
            def _(pe):
                for t in range(ET):
                    q = t % per_bank
                    mm = pe.matmul(bank[t // per_bank][:, q * RT:(q + 1) * RT], is_lo[:, t, :],
                                   is_hi_bf[:, t, :], start=True, stop=True)
                    if q == per_bank - 1 or t == ET - 1:
                        mm.then_inc(counted, 1)

            @block.vector
            def _(dve):
                for b in range(banks_n):
                    n = min(per_bank, ET - b * per_bank)
                    dve.wait_ge(counted, b + 1)
                    src = bank[b][:, 0:n * RT].rearrange("p (t h) -> p h t", h=RT)
                    g.link(dve, dve.tensor_copy(count[:, :, b * per_bank:b * per_bank + n], src))
                dve.tensor_reduce(total[:, :], count[:, :, :], AX.X, ALU.add)
                g.link(dve, dve.tensor_tensor_scan(run[:, :, :].rearrange("p h t -> p (h t)"),
                                                   count[:, :, :].rearrange("p h t -> p (h t)"), zeros[:, :],
                                                   0.0, ALU.add, ALU.add))

        with ExitStack() as inner:
            bank = inner.enter_context(nc.psum_tensor("node_bank", [P, 2, 512], F32))
            summed = inner.enter_context(g.semaphore("node_summed"))
            block = inner.enter_context(nc.Block(no_gpsimd_drain=True))

            @block.tensor
            def _(pe):
                pe.matmul(bank[:, 0, 0:RT], g.ones[:, :], total[:, :], start=True, stop=True)
                pe.matmul(bank[:, 1, 0:RT], g.below[:, :], total[:, :], start=True,
                          stop=True).then_inc(summed, 1)

            @block.vector
            def _(dve):
                dve.wait_ge(summed, 1)
                steps = [
                    lambda: dve.tensor_scalar(node_tot[:, :], bank[:, 0, 0:RT], float(P - 1), None, ALU.add),
                    lambda: dve.tensor_copy(tiles_i[:, :], node_tot[:, :]),
                    lambda: dve.tensor_scalar(tiles_i[:, :], tiles_i[:, :], 7, None, ALU.logical_shift_right),
                    lambda: dve.tensor_copy(tiles[:, :], tiles_i[:, :]),
                    lambda: dve.tensor_tensor_scan(tiles_end[:, :], tiles[:, :], zeros[:, 0:RT], 0.0,
                                                   ALU.add, ALU.add),
                    lambda: dve.tensor_tensor(first_tile[:, :], tiles_end[:, :], tiles[:, :], ALU.subtract),
                    lambda: dve.scalar_tensor_tensor(base[:, :], first_tile[:, :], float(P), bank[:, 1, 0:RT],
                                                     ALU.mult, ALU.add),
                    lambda: dve.tensor_tensor(before[:, :], run[:, :, ET - 1], total[:, :], ALU.subtract),
                    lambda: dve.tensor_tensor(base[:, :], base[:, :], before[:, :], ALU.subtract),
                    lambda: dve.tensor_tensor(run[:, :, :], run[:, :, :], count[:, :, :], ALU.subtract),
                    lambda: dve.tensor_tensor(run[:, :, :], run[:, :, :],
                                              base[:, :].unsqueeze(2).broadcast_to([P, RT, ET]), ALU.add),
                    lambda: dve.tensor_copy(start_i[:, 0, :], run[:, :, :].rearrange("p h t -> p (h t)")),
                    lambda: dve.tensor_scalar(start_i[:, 1, :], start_i[:, 0, :], P - 1, None, ALU.bitwise_and),
                    lambda: dve.tensor_scalar(start_i[:, 0, :], start_i[:, 0, :], 7, None,
                                              ALU.logical_shift_right),
                    lambda: dve.tensor_copy(start[:, :, 0, :],
                                            start_i[:, 0, :].rearrange("p (h t) -> p t h", h=RT)),
                    lambda: dve.tensor_copy(start[:, :, 1, :],
                                            start_i[:, 1, :].rearrange("p (h t) -> p t h", h=RT)),
                    lambda: dve.tensor_scalar(tile_node[0:1, :], g.tile_numbers[0:1, :], first_tile[0:1, 1:2],
                                              None, ALU.is_ge),
                ]
                for h in range(2, RT):
                    steps.append(lambda h=h: dve.scalar_tensor_tensor(
                        tile_node[0:1, :], g.tile_numbers[0:1, :], first_tile[0:1, h:h + 1],
                        tile_node[0:1, :], ALU.is_ge, ALU.add))
                for make in steps:
                    g.link(dve, make())

        transposes(g, "lo_turn", [is_lo[:, t, :] for t in range(ET)],
                   lambda j, n: is_lo_t[:, j * 8:j * 8 + n, :], BF16, per_bank=8, by="scalar")

        per_bank = 25
        banks_n = -(-ET // per_bank)
        with ExitStack() as inner:
            bank = [inner.enter_context(nc.psum_tensor(f"pick_bank{i}", [P, 512], F32)) for i in range(banks_n)]
            keyed = [inner.enter_context(g.semaphore(f"keyed{i}")) for i in range(2)]
            ranked = inner.enter_context(g.semaphore("ranked"))
            found = inner.enter_context(g.semaphore("found"))
            block = inner.enter_context(nc.Block(no_gpsimd_drain=True))
            chunks = [(a, min(KT, ET - a)) for a in range(0, ET, KT)]

            @block.tensor
            def _(pe):
                for t in range(ET):
                    q = t % per_bank
                    mm = pe.matmul(bank[t // per_bank][:, q * 2 * RT:(q + 1) * 2 * RT], is_lo_t[:, t, :],
                                   start[:, t, :, :].rearrange("p a h -> p (a h)"), start=True, stop=True)
                    if q == per_bank - 1 or t == ET - 1:
                        mm.then_inc(found, 1)

            @block.sync
            def _(sp):
                for i, (a, n) in enumerate(chunks):
                    if i >= 2:
                        sp.wait_ge(ranked, i - 1)
                    sp.dma_start(keys[:, i % 2, 0:n * P],
                                 src_by_tile_d[:, a * P:(a + n) * P].partition_broadcast(P)
                                 ).then_inc(keyed[i % 2], 16)

            @block.vector
            def _(dve):
                for b in range(banks_n):
                    n = min(per_bank, ET - b * per_bank)
                    ts = slice(b * per_bank, b * per_bank + n)
                    dve.wait_ge(found, b + 1)
                    dve.tensor_tensor(picked[:, ts, :, :],
                                      bank[b][:, 0:n * 2 * RT].rearrange("p (t a h) -> p t a h", a=2, h=RT),
                                      is_hi[:, ts, :].unsqueeze(2).broadcast_to([P, n, 2, RT]), ALU.mult)
                g.link(dve, dve.memset(rank[:, :], 0.0))
                for i, (a, n) in enumerate(chunks):
                    dve.wait_ge(keyed[i % 2], 16 * (i // 2 + 1))
                    for t in range(a, a + n):
                        ins = dve.scalar_tensor_tensor(same[:, :], keys[:, i % 2, (t - a) * P:(t - a + 1) * P],
                                                       src_f[:, t:t + 1], g.above[:, :], ALU.is_equal, ALU.mult,
                                                       accum_out=rank[:, t:t + 1])
                        g.link(dve, ins)
                    dve.memset(same[:, 0:1], 0.0).then_inc(ranked, 1)
                    g.link(dve, dve.memset(same[:, 1:2], 0.0))
                g.link(dve, dve.tensor_reduce(digits[:, :, :], picked[:, :, :, :], AX.X, ALU.add))
                g.link(dve, dve.scalar_tensor_tensor(pos[:, :], digits[:, :, 0], float(P), digits[:, :, 1],
                                                     ALU.mult, ALU.add))
                g.link(dve, dve.tensor_tensor(pos[:, :], pos[:, :], rank[:, :], ALU.add))
                dve.tensor_copy(pos_i[:, :], pos[:, :])

        with g.semaphore("scattered") as scattered, nc.Block() as block:
            @block.gpsimd
            def _(pool):
                for t in range(ET):
                    pool.indirect_dma_start(
                        table, bass.IndirectOffsetOnAxis(ap=pos_i[:, t:t + 1], axis=0),
                        edge[:, t, :], None).then_inc(scattered, 16)
                pool.wait_ge(scattered, 16 * ET)


def wait_apart(eng, passed, sem, value):
    eng.wait_ge(sem, value)
    eng.sem_inc(passed, 1)


def edge_scores(g, sorted_e, q_table, k_table, score):
    nc = g.nc
    R = 4
    with ExitStack() as ctx:
        idx = ctx.enter_context(nc.sbuf_tensor("score_idx", [P, R, 2], I32))
        q_rows = ctx.enter_context(nc.sbuf_tensor("q_rows", [P, R, C], F32))
        k_rows = ctx.enter_context(nc.sbuf_tensor("k_rows", [P, R, C], F32))
        free = ctx.enter_context(g.semaphore("score_free"))
        passed = ctx.enter_context(g.semaphore("score_passed"))
        indexed = ctx.enter_context(g.semaphore("score_indexed"))
        gathered = [ctx.enter_context(g.semaphore(f"score_gathered{i}")) for i in range(R)]
        multiplied = ctx.enter_context(g.semaphore("score_multiplied"))
        block = ctx.enter_context(nc.Block())

        @block.gpsimd
        def _(pool):
            with pool.Fori(0, ST - R + 1, R) as t0:
                for i in range(R):
                    t = t0 + i
                    wait_apart(pool, passed, free, t + 1)
                    pool.tensor_copy(idx[:, i, :], sorted_e[:, bass.ds(t, 1), 1:3].bitcast(I32)
                                     .rearrange("p a f -> p (a f)")).then_inc(indexed, 1)
                    wait_apart(pool, passed, indexed, t + 1)
                    for rows, table, f in ((q_rows, q_table, 0), (k_rows, k_table, 1)):
                        pool.indirect_dma_start(rows[:, i, :], None, table,
                                                bass.IndirectOffsetOnAxis(ap=idx[:, i, f:f + 1], axis=0)
                                                ).then_inc(gathered[i], 16)

        @block.vector
        def _(dve):
            for i in range(R):
                dve.memset(q_rows[:, i, 0:1], 0.0).then_inc(free, 1)
            with dve.Fori(0, ST - R + 1, R) as t0:
                for i in range(R):
                    t = t0 + i
                    dve.wait_ge(gathered[i], t0 * (32 // R) + 32)
                    dve.tensor_tensor(q_rows[:, i, :], q_rows[:, i, :], k_rows[:, i, :],
                                      ALU.mult).then_inc(multiplied, 1)
                    dve.wait_ge(multiplied, t + 1)
                    dve.tensor_reduce(score[:, bass.ds(t, 1), :].rearrange("p a h -> p (a h)"),
                                      q_rows[:, i, :].rearrange("p (h d) -> p h d", h=H), AX.X,
                                      ALU.add).then_inc(free, 1)


def running_max(g, tag, score, start, peak, openness):
    nc = g.nc
    back = tag == "back"
    turn = (lambda ap: ap[:, ::-1]) if back else (lambda ap: ap)
    with ExitStack() as ctx:
        def sb(name, shape):
            return ctx.enter_context(nc.sbuf_tensor(f"{tag}_{name}", shape, F32))

        penalty = sb("penalty", [P, H, ST])
        ends = sb("ends", [P, 2, H])
        ends_t = sb("ends_t", [H, 2, P])
        state = sb("state", [H, P])
        carry_t = sb("carry_t", [H, P])
        carry = sb("carry", [P, H])
        on_vector(g, [
            lambda dve: dve.tensor_copy(penalty[:, :, :], start[:, :].unsqueeze(1).broadcast_to([P, H, ST])),
            lambda dve: dve.memset(penalty[:, :, 0:1], -BIG),
            lambda dve: dve.tensor_tensor_scan(peak[:, :, :].rearrange("p h t -> p (h t)"),
                                               penalty[:, :, :].rearrange("p h t -> p (h t)"),
                                               score[:, :, :].rearrange("p h t -> p (h t)"),
                                               0.0, ALU.add, ALU.max),
            lambda dve: dve.tensor_tensor_scan(openness[:, :], start[:, :], start[:, :], 0.0, ALU.min, ALU.min),
            lambda dve: dve.tensor_copy(ends[:, 0, :], peak[:, :, ST - 1]),
            lambda dve: dve.tensor_copy(ends[:, 1, :], openness[:, ST - 1:ST].broadcast_to([P, H])),
        ])
        transposes(g, f"{tag}_ends", [ends[:, 0, :], ends[:, 1, :]], lambda j, n: ends_t[:, :, :])
        shifted = turn(carry_t[:, :])
        on_vector(g, [
            lambda dve: dve.tensor_tensor_scan(state[:, :], turn(ends_t[:, 1, :]), turn(ends_t[:, 0, :]),
                                               -BIG, ALU.add, ALU.max),
            lambda dve: dve.memset(carry_t[:, :], -BIG),
            lambda dve: dve.tensor_copy(shifted[:, 1:P], state[:, 0:P - 1]),
        ])
        with nc.psum_tensor(f"{tag}_carry_bank", [P, H], F32) as bank, \
                g.semaphore(f"{tag}_carry_turned") as turned, nc.Block(no_gpsimd_drain=True) as block:
            @block.tensor
            def _(pe):
                pe.transpose(bank[:, :], carry_t[:, :], g.ident[0:H, 0:H]).then_inc(turned, 1)

            @block.vector
            def _(dve):
                dve.wait_ge(turned, 1)
                g.link(dve, dve.tensor_copy(carry[:, :], bank[:, :]))
                g.link(dve, dve.tensor_tensor(penalty[:, :, :],
                                              openness[:, :].unsqueeze(1).broadcast_to([P, H, ST]),
                                              carry[:, :].unsqueeze(2).broadcast_to([P, H, ST]), ALU.add))
                dve.tensor_tensor(peak[:, :, :], peak[:, :, :], penalty[:, :, :], ALU.max)


def segment_softmax_weights(g, sorted_e, score, table, p_table):
    nc = g.nc
    with ExitStack() as ctx:
        def sb(name, shape, dt=F32):
            return ctx.enter_context(nc.sbuf_tensor(name, shape, dt))

        key = sb("key", [P, ST + 2])
        edge_key_i = sb("edge_key_i", [P, 2], I32)
        start_f = sb("start_f", [P, ST])
        start_b = sb("start_b", [P, ST])
        open_f = sb("open_f", [P, ST])
        open_b = sb("open_b", [P, ST])
        s_f = sb("s_f", [P, H, ST])
        s_b = sb("s_b", [P, H, ST])
        peak_f = sb("peak_f", [P, H, ST])
        peak_b = sb("peak_b", [P, H, ST])
        weight = sb("weight", [P, ST, H])
        rows = table.rearrange("(p t) f -> p t f", p=P)
        with g.semaphore("key_cleared") as cleared, g.semaphore("keys_in") as keys_in, nc.Block() as block:
            @block.vector
            def _(dve):
                dve.memset(edge_key_i[:, :], -1).then_inc(cleared, 1)

            @block.sync
            def _(sp):
                sp.wait_ge(cleared, 1)
                sp.dma_start(edge_key_i[1:P, 0:1].bitcast(F32), rows[0:P - 1, ST - 1, 1:2],
                             allow_slow_non_contiguous=True).then_inc(keys_in, 16)
                sp.dma_start(edge_key_i[0:P - 1, 1:2].bitcast(F32), rows[1:P, 0, 1:2],
                             allow_slow_non_contiguous=True).then_inc(keys_in, 16)
                sp.wait_ge(keys_in, 32)
        on_vector(g, [
            lambda dve: dve.tensor_copy(key[:, 1:ST + 1], sorted_e[:, :, 1].bitcast(I32)),
            lambda dve: dve.tensor_copy(key[:, 0:1], edge_key_i[:, 0:1]),
            lambda dve: dve.tensor_copy(key[:, ST + 1:ST + 2], edge_key_i[:, 1:2]),
            lambda dve: dve.tensor_tensor(start_f[:, :], key[:, 1:ST + 1], key[:, 0:ST], ALU.not_equal),
            lambda dve: dve.tensor_tensor(start_b[:, ::-1], key[:, 1:ST + 1], key[:, 2:ST + 2], ALU.not_equal),
            lambda dve: dve.tensor_scalar(start_f[:, :], start_f[:, :], -BIG, None, ALU.mult),
            lambda dve: dve.tensor_scalar(start_b[:, :], start_b[:, :], -BIG, None, ALU.mult),
            lambda dve: dve.scalar_tensor_tensor(s_f[:, :, :], score[:, :, :].rearrange("p t h -> p h t"),
                                                 float(D) ** -0.5,
                                                 sorted_e[:, :, 3:3 + H].rearrange("p t h -> p h t"),
                                                 ALU.mult, ALU.add),
            lambda dve: dve.tensor_copy(s_b[:, :, ::-1], s_f[:, :, :]),
        ])
        running_max(g, "forth", s_f, start_f, peak_f, open_f)
        running_max(g, "back", s_b, start_b, peak_b, open_b)
        on_vector(g, [
            lambda dve: dve.tensor_tensor(peak_f[:, :, :], peak_f[:, :, :], peak_b[:, :, ::-1], ALU.max),
            lambda dve: dve.tensor_tensor(s_f[:, :, :], s_f[:, :, :], peak_f[:, :, :], ALU.subtract),
        ])
        with g.semaphore("weighed") as weighed, g.semaphore("weights_out") as out, nc.Block() as block:
            @block.scalar
            def _(act):
                act.activation(weight[:, :, :].rearrange("p t h -> p h t"), s_f[:, :, :],
                               ACT.Exp).then_inc(weighed, 1)

            @block.sync
            def _(sp):
                sp.wait_ge(weighed, 1)
                sp.dma_start(p_table.rearrange("(p t) h -> p (t h)", p=P),
                             weight[:, :, :].rearrange("p t h -> p (t h)")).then_inc(out, 16)
                sp.wait_ge(out, 16)


def aggregate(g, name, lo, dst, tile_node, rows_table, width, weight, acc):
    nc = g.nc
    R = 4
    extra = H if weight is not None else 1
    W = width + extra
    with ExitStack() as ctx:
        def sb(n, shape, dt=F32):
            return ctx.enter_context(nc.sbuf_tensor(f"{name}_{n}", shape, dt))

        def sem(n):
            return ctx.enter_context(g.semaphore(f"{name}_{n}"))

        idx = sb("idx", [P, R], I32)
        rows = sb("rows", [P, R, W])
        onehot = sb("onehot", [P, R, P])
        banks = [ctx.enter_context(nc.psum_tensor(f"{name}_bank{i}", [P, 1024], F32)) for i in range(R)]
        free, indexed, ready, summed, added = sem("free"), sem("indexed"), sem("ready"), sem("summed"), sem("added")
        passed = sem("passed")
        gathered = [sem(f"gathered{i}") for i in range(R)]
        block = ctx.enter_context(nc.Block())

        @block.gpsimd
        def _(pool):
            with pool.Fori(0, ST - R + 1, R) as t0:
                for i in range(R):
                    t = t0 + i
                    wait_apart(pool, passed, free, t + 1)
                    pool.tensor_copy(idx[:, i:i + 1], dst[:, bass.ds(t, 1)]).then_inc(indexed, 1)
                    wait_apart(pool, passed, indexed, t + 1)
                    pool.indirect_dma_start(rows[:, i, 0:width], None, rows_table,
                                            bass.IndirectOffsetOnAxis(ap=idx[:, i:i + 1], axis=0)
                                            ).then_inc(gathered[i], 16)

        @block.vector
        def _(dve):
            g.link(dve, dve.memset(acc[:, :], 0.0))
            for i in range(R):
                dve.memset(rows[:, i, width:], 1.0).then_inc(free, 1)

            def prepare(t0, i):
                t = t0 + i
                if weight is None:
                    dve.wait_ge(free, t + 1)
                else:
                    dve.wait_ge(gathered[i], t0 * (16 // R) + 16)
                    w_t = weight[:, bass.ds(t, 1), :].rearrange("p a h -> p (a h)")
                    dve.tensor_tensor(rows[:, i, 0:width].rearrange("p (h d) -> p h d", h=H),
                                      rows[:, i, 0:width].rearrange("p (h d) -> p h d", h=H),
                                      w_t.unsqueeze(2).broadcast_to([P, H, D]), ALU.mult)
                    dve.tensor_copy(rows[:, i, width:], w_t)
                dve.tensor_scalar(onehot[:, i, :], g.numbers_f[:, :], lo[:, bass.ds(t, 1)], None,
                                  ALU.is_equal).then_inc(ready, 1)

            def add(t0, i):
                t = t0 + i
                node = dve.value_load(tile_node[0:1, bass.ds(t, 1)], min_val=0, max_val=RT - 1)
                dve.wait_ge(summed, t + 1)
                dve.wait_ge(free, t + R)
                at = acc[:, bass.ds(node * W, W)]
                dve.tensor_tensor(at, at, banks[i][:, 0:W], ALU.add).then_inc(free, 1)

            with dve.Fori(0, ST - R + 1, R) as t0:
                prepare(t0, 0)
                for i in range(1, R):
                    prepare(t0, i)
                    add(t0, i - 1)
                add(t0, R - 1)

        @block.tensor
        def _(pe):
            with pe.Fori(0, ST - R + 1, R) as t0:
                for i in range(R):
                    pe.wait_ge(ready, t0 + i + 1)
                    if weight is None:
                        pe.wait_ge(gathered[i], t0 * (16 // R) + 16)
                    for a in range(0, W, 512):
                        b = min(W, a + 512)
                        mm = pe.matmul(banks[i][:, a:b], onehot[:, i, :], rows[:, i, a:b], start=True, stop=True)
                    mm.then_inc(summed, 1)


def kernel_body(nc, d, out):
    g = Ctx(nc)
    with ExitStack() as life:
        def sb(name, shape, dt=F32, scope=life):
            return scope.enter_context(nc.sbuf_tensor(name, shape, dt))

        def dram(name, shape, dt=F32):
            return nc.dram_tensor(name, shape, dt).ap()

        g.dve_chain = life.enter_context(nc.semaphore("dve_chain"))
        g.ident = sb("ident", [P, P])
        g.ident_bf = sb("ident_bf", [P, P], BF16)
        g.below = sb("below", [P, P])
        g.above = sb("above", [P, P])
        g.mean = sb("mean", [P, P])
        g.ones = sb("ones", [P, P])
        g.numbers = sb("numbers", [P, P], I32)
        g.numbers_f = sb("numbers_f", [P, P])
        g.sel = sb("sel", [8, 8, P])
        tile_node = sb("tile_node", [1, ST], I32)
        lo_t = sb("lo_t", [P, ST])
        dst_t = sb("dst_t", [P, ST], I32)

        q_table = dram("q_table", (NP, C))
        k_table = dram("k_table", (NP, C))
        v_table = dram("v_table", (NP, C))
        r_table = dram("r_table", (NP, 256))
        table = dram("edge_table", (ST * P, FIELDS))
        p_table = dram("p_table", (ST * P, H))

        constants(g)
        with ExitStack() as s0:
            tile_f = sb("tile_f", [1, ST], scope=s0)
            g.tile_numbers = sb("tile_numbers", [1, ST], scope=s0)
            tile_i = sb("tile_i", [1, ST], I32, scope=s0)
            with nc.Block() as block:
                @block.gpsimd
                def _(pool):
                    pool.iota(tile_i[:, :], pattern=[[1, ST]], base=0, channel_multiplier=0)
            on_vector(g, [lambda dve: dve.tensor_copy(g.tile_numbers[:, :], tile_i[:, :])])
            sort_edges(g, d["src"], d["dst"], d["attr"], d["src_by_tile"], table, tile_f)
            on_vector(g, [lambda dve: dve.tensor_copy(tile_node[:, :], tile_f[:, :])])

        x = sb("x", [P, KC, NP])
        xn = sb("xn", [P, KC, NP])
        transfer(g, "x_in", [(x[:, :, :].rearrange("p k n -> p (k n)"), d["x"])])
        att = ExitStack()
        agg = sb("agg", [P, RT * (C + H)], scope=att)
        g.end_phase()
        with ExitStack() as s0:
            z = sb("z", [P, KC, NP], scope=s0)
            wqkv = [sb(f"w{n}", [P, KC, C], scope=s0) for n in "qkv"]
            bqkv = [sb(f"b{n}", [P, C], scope=s0) for n in "qkv"]
            ln_gain = sb("ln_gain", [P, KC], scope=s0)
            ln_shift = sb("ln_shift", [P, KC], scope=s0)
            layer_norm(g, "ln0", x, xn, loads=[(ln_gain[:, :], d["ln_att_g"]), (ln_shift[:, :], d["ln_att_b"])])
            layer_norm(g, "ln0a", xn, z, ln_gain, ln_shift,
                       loads=[(w[:, :, :].rearrange("p k n -> p (k n)"), d[f"g_W{n}"]) for w, n in zip(wqkv, "qkv")]
                       + [(b[:, :], d[f"g_b{n}"].partition_broadcast(P)) for b, n in zip(bqkv, "qkv")])
            tables(g, "qkv", z, wqkv, [b[:, :] for b in bqkv], [q_table, k_table, v_table])
        with ExitStack() as s0:
            sorted_e = sb("sorted_e", [P, ST, FIELDS], scope=s0)
            score = sb("score", [P, ST, H], scope=s0)
            transfer(g, "sorted_in", [(sorted_e[:, :, :].rearrange("p t f -> p (t f)"),
                                       table.rearrange("(p t) f -> p (t f)", p=P))])
            edge_scores(g, sorted_e, q_table, k_table, score)
            segment_softmax_weights(g, sorted_e, score, table, p_table)
        with ExitStack() as s0:
            by_tile = sb("by_tile", [P, ST, FIELDS], scope=s0)
            weight = sb("weight_t", [P, ST, H], scope=s0)
            transfer(g, "by_tile_in", [(by_tile[:, :, :], table.rearrange("(t p) f -> p t f", p=P)),
                                       (weight[:, :, :], p_table.rearrange("(t p) h -> p t h", p=P))])
            on_vector(g, [lambda dve: dve.tensor_copy(lo_t[:, :], by_tile[:, :, 0]),
                          lambda dve: dve.tensor_copy(dst_t[:, :], by_tile[:, :, 2].bitcast(I32))])
            aggregate(g, "attend", lo_t, dst_t, tile_node, v_table, C, weight, agg)

        with ExitStack() as s0:
            acc = agg[:, :].rearrange("p (r w) -> p r w", r=RT)
            denom = sb("denom", [P, RT, H], scope=s0)
            none = sb("none", [P, RT, H], scope=s0)
            feat = sb("feat", [P, KC, NP], scope=s0)
            x2 = sb("x2", [P, KC, NP], scope=s0)
            wo = sb("wo", [P, KC, C], scope=s0)
            w1 = sb("w1", [P, KC, HID], scope=s0)
            w2 = sb("w2", [P, HID // P, C], scope=s0)
            bo = sb("bo", [P, KC], scope=s0)
            b1 = sb("b1", [P, HID // P], scope=s0)
            b2 = sb("b2", [P, KC], scope=s0)
            gain = sb("gain", [P, KC], scope=s0)
            shift = sb("shift", [P, KC], scope=s0)
            hid = sb("hid", [P, HID // P, NP], scope=s0)
            gate = sb("gate", [P, 2, 512], scope=s0)
            transfer(g, "wo_in", [(wo[:, :, :].rearrange("p k n -> p (k n)"), d["g_Wo"]), (bo[:, :], d["g_bo"]),
                                  (gain[:, :], d["ln_ff_g"]), (shift[:, :], d["ln_ff_b"]),
                                  (b1[:, :], d["g_b1"]), (b2[:, :], d["g_b2"])])
            on_vector(g, [
                lambda dve: dve.tensor_scalar(none[:, :, :], acc[:, :, C:], 0.0, None, ALU.is_equal),
                lambda dve: dve.tensor_tensor(denom[:, :, :], acc[:, :, C:], none[:, :, :], ALU.add),
                lambda dve: dve.reciprocal(denom[:, :, :], denom[:, :, :])] + [
                lambda dve, r=r: dve.tensor_tensor(
                    acc[:, r, 0:C].rearrange("p (h e) -> p h e", h=H),
                    acc[:, r, 0:C].rearrange("p (h e) -> p h e", h=H),
                    denom[:, r, :].unsqueeze(2).broadcast_to([P, H, D]), ALU.mult) for r in range(RT)])
            transposes(g, "agg_turn", [acc[:, r, k * P:(k + 1) * P] for r in range(RT) for k in range(KC)],
                       lambda j, n: feat[:, :, j * P:(j + 1) * P], per_bank=KC)

            def add_att(dve, n, bank):
                m, cs = where(n)
                return dve.scalar_tensor_tensor(x2[:, m, cs], bank, bo[:, m:m + 1], xn[:, m, cs], ALU.add, ALU.add)
            products(g, "wo_gemm", linear(wo, feat), add_att,
                     loads=[(w1[:, :, :].rearrange("p k n -> p (k n)"), d["g_W1"]),
                            (w2[:, :, :].rearrange("p k n -> p (k n)"), d["g_W2"])])
            layer_norm(g, "lnff", x2, feat, gain, shift, sq=hid[:, 0:KC, :])
            with ExitStack() as s1:
                banks = [s1.enter_context(nc.psum_tensor(f"ff1_bank{i}", [P, 512], F32)) for i in range(4)]
                summed = s1.enter_context(g.semaphore("ff1_summed"))
                gated = s1.enter_context(g.semaphore("ff1_gated"))
                emptied = s1.enter_context(g.semaphore("ff1_emptied"))
                groups = linear(w1, feat, HID)
                block = s1.enter_context(nc.Block(no_gpsimd_drain=True))

                @block.tensor
                def _(pe):
                    for n, terms in enumerate(groups):
                        if n >= 4:
                            pe.wait_ge(emptied, n - 3)
                        for i, (lhsT, rhs) in enumerate(terms):
                            mm = pe.matmul(banks[n % 4][:, 0:rhs.shape[-1]], lhsT, rhs, start=(i == 0),
                                           stop=(i == KC - 1))
                        mm.then_inc(summed, 1)

                @block.scalar
                def _(act):
                    for n in range(len(groups)):
                        m, cs = where(n)
                        w = cs.stop - cs.start
                        act.wait_ge(summed, n + 1)
                        if n >= 2:
                            act.wait_ge(emptied, n - 1)
                        act.activation(gate[:, n % 2, 0:w], banks[n % 4][:, 0:w], ACT.Sigmoid,
                                       bias=b1[:, m:m + 1]).then_inc(gated, 1)

                @block.vector
                def _(dve):
                    for n in range(len(groups)):
                        m, cs = where(n)
                        w = cs.stop - cs.start
                        dve.wait_ge(gated, n + 1)
                        dve.scalar_tensor_tensor(hid[:, m, cs], banks[n % 4][:, 0:w], b1[:, m:m + 1],
                                                 gate[:, n % 2, 0:w], ALU.add, ALU.mult).then_inc(emptied, 1)

            def add_ff(dve, n, bank):
                m, cs = where(n)
                return dve.scalar_tensor_tensor(x2[:, m, cs], bank, b2[:, m:m + 1], x2[:, m, cs], ALU.add, ALU.add)
            products(g, "ff2", linear(w2, hid, C, HID // P), add_ff)
            on_vector(g, [lambda dve: dve.tensor_tensor(x[:, :, :], x[:, :, :], x2[:, :, :], ALU.add)])

        att.close()
        g.end_phase()
        linear_attention_0(g, d, x, xn)
        g.end_phase()
        lstm(g, d, x, xn)
        g.end_phase()
        layer_1(g, d, x, xn, lo_t, dst_t, tile_node, r_table)
        with g.semaphore("result_out") as done, nc.Block() as block:
            @block.sync
            def _(sp):
                sp.dma_start(out, x[:, :, :].rearrange("p k n -> p (k n)")).then_inc(done, 16)
                sp.wait_ge(done, 16)


def linear_attention_0(g, d, x, xn):
    nc = g.nc
    with ExitStack() as s0:
        def sb(name, shape, dt=F32, scope=s0):
            return scope.enter_context(nc.sbuf_tensor(name, shape, dt))

        wa = sb("m_wa", [P, KC, C])
        wb = sb("m_wb", [P, KC, C])
        wc = sb("m_wc", [P, KC, C])
        rows = sb("m_rows", [P, RT, C])
        feat = sb("m_feat", [P, KC, NP])
        v = sb("m_v", [P, RT, C])
        qt = sb("m_qt", [P, KC, NP])
        context = sb("m_context", [P, KC, C])
        small = sb("m_small", [P, 3, RT])
        kmax = sb("m_kmax", [P, KC])
        ksum = sb("m_ksum", [P, KC])
        flat = lambda w: w[:, :, :].rearrange("p k n -> p (k n)")
        transfer(g, "m_w", [(flat(wa), d["m_Wq"]), (flat(wb), d["m_Wk"]), (flat(wc), d["m_Wv"])])
        products(g, "m_q", rows_of(wa, xn), lambda e, n, bank: e.activation(rows[:, n, :], bank, ACT.Copy),
                 by="scalar")
        products(g, "m_k", linear(wb, xn),
                 lambda e, n, bank: e.activation(feat[:, where(n)[0], where(n)[1]], bank, ACT.Copy),
                 by="scalar", loads=[(flat(wa), d["m_W1"])])
        products(g, "m_v", rows_of(wc, xn), lambda e, n, bank: e.activation(v[:, n, :], bank, ACT.Copy),
                 by="scalar", loads=[(flat(wb), d["m_W2"])])
        on_vector(g, [
            lambda dve: dve.tensor_reduce(small[:, 0, :], rows[:, :, :], AX.X, ALU.max, negate=True),
            lambda dve: dve.tensor_reduce(kmax[:, :], feat[:, :, 0:N], AX.X, ALU.max, negate=True),
            lambda dve: dve.memset(small[:, 1, :], 0.0)])
        on_scalar(g, "m_exp", [
            lambda act, r=r: act.activation(rows[:, r, :], rows[:, r, :], ACT.Exp, bias=small[:, 0, r:r + 1],
                                            accum_out=small[:, 1, r:r + 1]) for r in range(RT)] + [
            lambda act, k=k: act.activation(feat[:, k, 0:N], feat[:, k, 0:N], ACT.Exp, bias=kmax[:, k:k + 1],
                                            accum_out=ksum[:, k:k + 1]) for k in range(KC)])
        on_vector(g, [
            lambda dve: dve.memset(feat[:, :, N:], 0.0),
            lambda dve: dve.reciprocal(ksum[:, :], ksum[:, :]),
            lambda dve: dve.reciprocal(small[:, 2, :], small[:, 1, :])] + [
            lambda dve, r=r: dve.tensor_scalar(rows[:, r, :], rows[:, r, :], small[:, 2, r:r + 1],
                                               float(C) ** -0.5, ALU.mult, ALU.mult) for r in range(RT)])
        transposes(g, "m_q_turn", [rows[:, r, k * P:(k + 1) * P] for r in range(RT) for k in range(KC)],
                   lambda j, n: qt[:, :, j * P:(j + 1) * P], per_bank=KC)
        transposes(g, "m_k_turn", [feat[:, k, r * P:(r + 1) * P] for r in range(RT) for k in range(KC)],
                   lambda j, n: rows[:, j, :].rearrange("p (k n) -> p k n", k=KC), per_bank=KC)
        products(g, "m_context",
                 [[(rows[:, r, k * P:(k + 1) * P], v[:, r, :]) for r in range(RT)] for k in range(KC)],
                 lambda e, n, bank: e.tensor_scalar(context[:, n, :], bank, ksum[:, n:n + 1], None, ALU.mult))
        y, u = v[:, :, :].rearrange("p r c -> p (r c)").rearrange("p (k n) -> p k n", k=KC), feat

        def residual(dve, n, bank):
            m, cs = where(n)
            return dve.tensor_tensor(y[:, m, cs], bank, xn[:, m, cs], ALU.add)
        products(g, "m_attn", linear(context, qt), residual)
        products(g, "m_w1", linear(wa, y),
                 lambda e, n, bank: e.tensor_copy(u[:, where(n)[0], where(n)[1]], bank))

        def add_out(dve, n, bank):
            m, cs = where(n)
            return dve.tensor_tensor(x[:, m, cs], bank, x[:, m, cs], ALU.add)
        products(g, "m_w2", linear(wb, u), add_out)
        on_vector(g, [lambda dve: dve.tensor_tensor(x[:, :, :], x[:, :, :], y, ALU.add)])


GATES = 4
M16 = KC * GATES
H_SCALE = 2.0 ** 13


def lstm(g, d, x, h):
    nc = g.nc
    with ExitStack() as s0:
        def sb(name, shape, dt=F32, scope=s0):
            return scope.enter_context(nc.sbuf_tensor(name, shape, dt))

        xp = sb("l_xp", [P, NP, M16])
        w16 = sb("l_w16", [P, 2, KC, M16, P], F16)
        scale = sb("l_scale", [P, 3])
        scale_x = sb("l_scale_x", [P, 2])
        with ExitStack() as s1:
            wh = sb("l_wh", [P, KC, M16, P], scope=s1)
            top = sb("l_top", [P, 2], scope=s1)
            bits = sb("l_bits", [P, 1], I32, scope=s1)
            expo = sb("l_expo", [P, 1], scope=s1)
            squares = xp[:, :, :].rearrange("p n m -> p (n m)")[:, 0:KC * NP].rearrange("p (k n) -> p k n", k=KC)
            layer_norm(g, "l_ln", x, h, sq=squares,
                       loads=[(wh[:, :, :, :].rearrange("p k m n -> p (k m n)"), d["l_Wh"])])
            on_vector(g, [
                lambda dve: dve.tensor_reduce(top[:, 0:1], wh[:, :, :, :].rearrange("p k m n -> p (k m n)"), AX.X,
                                              ALU.max, apply_absolute_value=True),
                lambda dve: dve.tensor_scalar(top[:, 0:1], top[:, 0:1], 2.0 ** -20, None, ALU.max)])
            with nc.Block() as block:
                @block.gpsimd
                def _(pool):
                    pool.partition_all_reduce(top[:, 1:2], top[:, 0:1], P, RMAX)
            on_vector(g, [
                lambda dve: dve.tensor_scalar(bits[:, :], top[:, 1:2].bitcast(I32), 23, None,
                                              ALU.logical_shift_right),
                lambda dve: dve.tensor_copy(expo[:, :], bits[:, :]),
                lambda dve: dve.tensor_scalar(expo[:, :], expo[:, :], -1.0, 127.0 + 127 + 13, ALU.mult, ALU.add),
                lambda dve: dve.tensor_copy(bits[:, :], expo[:, :]),
                lambda dve: dve.tensor_scalar(scale[:, 1:2].bitcast(I32), bits[:, :], 23, None,
                                              ALU.logical_shift_left),
                lambda dve: dve.tensor_scalar(scale[:, 0:1], scale[:, 1:2], 0.5, None, ALU.mult),
                lambda dve: dve.tensor_scalar(expo[:, :], expo[:, :], -1.0, 127.0 + 127 - 13, ALU.mult, ALU.add),
                lambda dve: dve.tensor_copy(bits[:, :], expo[:, :]),
                lambda dve: dve.tensor_scalar(scale[:, 2:3].bitcast(I32), bits[:, :], 23, None,
                                              ALU.logical_shift_left),
                lambda dve: dve.tensor_scalar(scale_x[:, :], scale[:, 0:2], H_SCALE, None, ALU.mult)])
            parts = []
            for part in range(2):
                for k in range(KC):
                    for gate in range(GATES):
                        v = wh[:, k, :, :].rearrange("p (j q) n -> p j q n", q=GATES)[:, :, gate, :]
                        o = w16[:, :, k, :, :].rearrange("p a (j q) n -> p a j q n", q=GATES)[:, :, :, gate, :]
                        s = scale[:, 0:1] if gate < 3 else scale[:, 1:2]
                        if part == 0:
                            parts.append(lambda dve, o=o, v=v, s=s: dve.tensor_scalar(
                                o[:, 0], v, s, None, ALU.mult))
                        else:
                            parts.append(lambda dve, o=o, v=v, s=s: dve.scalar_tensor_tensor(
                                o[:, 1], v, s, o[:, 0], ALU.mult, ALU.subtract))
            on_vector(g, parts)
        with ExitStack() as s1:
            wx = sb("l_wx", [P, KC, GATES * C], scope=s1)
            bias = sb("l_bias", [P, M16], scope=s1)
            transfer(g, "l_wx_in", [(wx[:, :, :].rearrange("p k n -> p (k n)"), d["l_Wx"]), (bias[:, :], d["l_b"])])
            groups = [[(wx[:, k, gate * C + j * P:gate * C + (j + 1) * P], h[:, k, a:a + n]) for k in range(KC)]
                      for j in range(KC) for gate in range(GATES) for a, n in COLS]

            def scaled(dve, n, bank):
                m, cs = where(n)
                s = scale_x[:, 0:1] if m % GATES < 3 else scale_x[:, 1:2]
                return dve.tensor_scalar(xp[:, cs, m], bank, bias[:, m:m + 1], s, ALU.add, ALU.mult)
            products(g, "l_xproj", groups, scaled)

        hp = sb("l_hp", [P, 2, KC, 2], F16)
        z = sb("l_z", [P, 2, 2, 8])
        th = sb("l_th", [P, 2, 2, 8])
        gi = sb("l_gi", [P, KC])
        gf = sb("l_gf", [P, KC])
        go = sb("l_go", [P, KC])
        c = sb("l_c", [P, KC])
        tc = sb("l_tc", [P, KC])
        banks = [[s0.enter_context(nc.psum_tensor(f"l_bank{i}{q}", [P, 512], F32)) for q in range(2)]
                 for i in range(2)]

        def pair(name):
            return [s0.enter_context(g.semaphore(f"l_{name}{q}")) for q in range(2)]

        s_gates, s_sum, s_tanh, s_terms, s_cell, s_tcell, s_full, s_h = [
            pair(n) for n in ("gates", "sum", "tanh", "terms", "cell", "tcell", "full", "h")]
        block = s0.enter_context(nc.Block(no_gpsimd_drain=True))

        @block.tensor
        def _(pe):
            def step(t, par):
                def block_of(k, ms, signal=None):
                    for m in ms:
                        q, c0 = m // 8, 2 * (m % 8)
                        for part in range(2):
                            mm = pe.matmul(banks[par][q][:, c0:c0 + 2], w16[:, part, k, m, :], hp[:, par, k, :],
                                           start=False, stop=signal is not None, skip_group_check=True)
                    if signal is not None:
                        mm.then_inc(signal, 1)

                for q in range(2):
                    pe.matmul(banks[par][q][:, 0:16].rearrange("p (m two) -> p m two", two=2)[:, :, 0],
                              g.ident[:, :], xp[:, bass.ds(t, 1), 8 * q:8 * q + 8].rearrange("p a m -> p (a m)"),
                              start=True, stop=False, skip_group_check=True)
                pe.wait_ge(s_h[0], t + 1)
                block_of(0, range(0, 8))
                block_of(1, range(0, 8))
                block_of(0, range(8, 12))
                pe.wait_ge(s_h[1], t + 1)
                block_of(2, range(0, 8))
                block_of(3, range(0, 8), s_gates[0])
                block_of(0, range(12, 16))
                block_of(1, range(8, 16))
                block_of(2, range(8, 16))
                block_of(3, range(8, 16), s_gates[1])
            with pe.Fori(0, N, 2) as t:
                step(t, 0)
                step(t + 1, 1)

        @block.scalar
        def _(act):
            act.preload_act_table(ACT.Tanh)

            def step(t, par):
                for q in range(2):
                    act.wait_ge(s_sum[q], t + 1)
                    act.activation(th[:, par, q, :], z[:, par, q, :], ACT.Tanh,
                                   scale=scale[:, 2:3]).then_inc(s_tanh[q], 1)
                    act.wait_ge(s_cell[q], t + 1)
                    act.activation(tc[:, 2 * q:2 * q + 2], c[:, 2 * q:2 * q + 2], ACT.Tanh,
                                   scale=0.5).then_inc(s_tcell[q], 1)
            with act.Fori(0, N, 2) as t:
                step(t, 0)
                step(t + 1, 1)

        @block.vector
        def _(dve):
            g.link(dve, dve.memset(c[:, :], 0.0))
            dve.memset(hp[:, 0, 0:2, :], 0.0).then_inc(s_h[0], 1)
            dve.memset(hp[:, 0, 2:4, :], 0.0).then_inc(s_h[1], 1)

            def step(t, par):
                for q in range(2):
                    two = slice(2 * q, 2 * q + 2)
                    gate = th[:, par, q, :].rearrange("p (j q) -> p j q", q=GATES)
                    dve.wait_ge(s_gates[q], t + 1)
                    dve.tensor_reduce(z[:, par, q, :],
                                      banks[par][q][:, 0:16].rearrange("p (m two) -> p m two", two=2), AX.X,
                                      ALU.add).then_inc(s_sum[q], 1)
                    dve.wait_ge(s_tanh[q], t + 1)
                    dve.scalar_tensor_tensor(gi[:, two], gate[:, :, 1], 1.0, gate[:, :, 3], ALU.add, ALU.mult)
                    dve.scalar_tensor_tensor(gf[:, two], gate[:, :, 0], 1.0, c[:, two], ALU.add,
                                             ALU.mult).then_inc(s_terms[q], 1)
                    dve.tensor_scalar(go[:, two], gate[:, :, 2], H_SCALE / 2, H_SCALE / 2, ALU.mult, ALU.add)
                    dve.wait_ge(s_terms[q], t + 1)
                    dve.scalar_tensor_tensor(c[:, two], gf[:, two], 0.5, gi[:, two], ALU.mult,
                                             ALU.add).then_inc(s_cell[q], 1)
                    dve.wait_ge(s_tcell[q], t + 1)
                    dve.tensor_tensor(hp[:, 1 - par, two, 0], go[:, two], tc[:, two], ALU.mult)
                    dve.tensor_tensor(h[:, two, bass.ds(t, 1)].rearrange("p j a -> p (j a)"), go[:, two],
                                      tc[:, two], ALU.mult).then_inc(s_full[q], 1)
                    dve.wait_ge(s_full[q], t + 1)
                    dve.tensor_tensor(hp[:, 1 - par, two, 1],
                                      h[:, two, bass.ds(t, 1)].rearrange("p j a -> p (j a)"),
                                      hp[:, 1 - par, two, 0], ALU.subtract).then_inc(s_h[q], 1)
            with dve.Fori(0, N, 2) as t:
                step(t, 0)
                step(t + 1, 1)
            dve.wait_ge(s_h[1], N + 1)
            dve.scalar_tensor_tensor(x[:, :, 0:N], h[:, :, 0:N], 1.0 / H_SCALE, x[:, :, 0:N], ALU.mult, ALU.add)


def layer_1(g, d, x, xn, lo_t, dst_t, tile_node, r_table):
    nc = g.nc
    flat = lambda w: w[:, :, :].rearrange("p k n -> p (k n)")
    W = 257
    with ExitStack() as s0:
        def sb(name, shape, dt=F32, scope=s0):
            return scope.enter_context(nc.sbuf_tensor(name, shape, dt))

        w1 = sb("c_w1", [P, KC, 256])
        b1 = sb("c_b1", [P, 256])
        w2 = sb("c_w2", [P, 2, C])
        b2 = sb("c_b2", [1, C])
        r = sb("c_r", [P, RT, 256])
        rt = sb("c_rt", [P, 2, NP])
        edges_t = sb("c_edges_t", [1, NP])
        layer_norm(g, "ln1", x, xn, loads=[(flat(w1), d["c_W1"]), (b1[:, :], d["c_b1"].partition_broadcast(P)),
                                           (flat(w2), d["c_W2"]), (b2[:, :], d["c_b2"])])
        tables(g, "r", xn, [w1], [b1[:, :]], [r_table], relu=True)
        acc = sb("c_acc", [P, RT * W])[:, :]
        aggregate(g, "conv", lo_t, dst_t, tile_node, r_table, 256, None, acc)
        transfer(g, "r_in", [(r[:, :, :], r_table.rearrange("(r p) f -> p r f", p=P))])
        a3 = acc.rearrange("p (r w) -> p r w", w=W)
        on_vector(g, [lambda dve: dve.tensor_tensor(r[:, :, :], r[:, :, :], a3[:, :, 0:256], ALU.add),
                      lambda dve: dve.tensor_scalar(a3[:, :, 256:257], a3[:, :, 256:257], 1.0, None, ALU.add)])
        transposes(g, "c_turn", [r[:, i, k * P:(k + 1) * P] for i in range(RT) for k in range(2)],
                   lambda j, n: rt[:, :, j * P:(j + 1) * P], per_bank=2)
        transposes(g, "c_edges_turn", [a3[:, i, 256:257] for i in range(RT)],
                   lambda j, n: edges_t[:, j * 4 * P:(j * 4 + n) * P].rearrange("p (n m) -> p n m", m=P))
        groups = [[(w2[:, k, m * P:(m + 1) * P], rt[:, k, a:a + n]) for k in range(2)]
                  + [(b2[:, m * P:(m + 1) * P], edges_t[:, a:a + n])] for m in range(KC) for a, n in COLS]

        def add(dve, n, bank):
            m, cs = where(n)
            return dve.tensor_tensor(x[:, m, cs], bank, x[:, m, cs], ALU.add)
        products(g, "c_w2_gemm", groups, add)

    g.end_phase()
    with ExitStack() as s0:
        def sb(name, shape, dt=F32, scope=s0):
            return scope.enter_context(nc.sbuf_tensor(name, shape, dt))

        wq, wk, wv, wo = [sb(f"a_w{n}", [P, KC, C]) for n in "qkvo"]
        bk, bv = sb("a_bk", [P, C]), sb("a_bv", [P, C])
        bq, bo = sb("a_bq", [P, KC]), sb("a_bo", [P, KC])
        q, q_low = sb("a_q", [P, KC, NP]), sb("a_q_low", [P, KC, NP])
        k, k_low = sb("a_k", [P, RT, C]), sb("a_k_low", [P, RT, C])
        v = sb("a_v", [P, RT, C])
        kv, ks = sb("a_kv", [P, KC, P]), sb("a_ks", [P, KC, P])
        o, inv = q_low, xn
        transfer(g, "a_w", [(flat(w), d[f"a_W{n}"]) for w, n in ((wq, "q"), (wk, "k"), (wv, "v"), (wo, "o"))]
                 + [(bk[:, :], d["a_bk"].partition_broadcast(P)), (bv[:, :], d["a_bv"].partition_broadcast(P)),
                    (bq[:, :], d["a_bq"]), (bo[:, :], d["a_bo"])])

        def q_parts(dve, n, bank):
            m, cs = where(n)
            dve.tensor_scalar(q_low[:, m, cs], bank, bq[:, m:m + 1], 0.0, ALU.add, ALU.min)
            return dve.tensor_scalar(q[:, m, cs], bank, bq[:, m:m + 1], 0.0, ALU.add, ALU.max)
        products(g, "a_q_gemm", linear(wq, xn), q_parts)
        products(g, "a_k_gemm", rows_of(wk, xn),
                 lambda e, n, bank: e.tensor_tensor(k[:, n, :], bank, bk[:, :], ALU.add))
        products(g, "a_v_gemm", rows_of(wv, xn),
                 lambda e, n, bank: e.tensor_tensor(v[:, n, :], bank, bv[:, :], ALU.add))
        on_vector(g, [lambda dve: dve.tensor_scalar(k_low[:, :, :], k[:, :, :], 0.0, None, ALU.min),
                      lambda dve: dve.tensor_scalar(k[:, :, :], k[:, :, :], 0.0, None, ALU.max)])
        on_scalar(g, "a_exp", [lambda act: act.activation(k_low[:, :, :], k_low[:, :, :], ACT.Exp),
                               lambda act: act.activation(q_low[:, :, :], q_low[:, :, :], ACT.Exp)])
        on_vector(g, [lambda dve: dve.tensor_tensor(k[:, :, :], k[:, :, :], k_low[:, :, :], ALU.add),
                      lambda dve: dve.tensor_tensor(q[:, :, :], q[:, :, :], q_low[:, :, :], ALU.add),
                      lambda dve: dve.memset(kv[:, :, :], 0.0), lambda dve: dve.memset(ks[:, :, :], 0.0)])
        true = [P] * (RT - 1) + [LAST]
        pairs = [[(k[0:n, i, j * P:(j + 1) * P], v[0:n, i, j * P:(j + 1) * P]) for i, n in enumerate(true)]
                 for j in range(KC)]
        sums = [[(k[0:n, i, j * P:(j + 1) * P], g.ones[0:n, :]) for i, n in enumerate(true)] for j in range(KC)]

        def diagonal(dve, n, bank):
            dst = (kv if n < KC else ks)[:, n % KC, :]
            dve.tensor_copy(dst[0:D, 0:D], bank[0:D, 0:D])
            return dve.tensor_copy(dst[D:P, D:P], bank[D:P, D:P])
        products(g, "a_kv_gemm", pairs + sums, diagonal)
        over = [[(kv[:, j, :], q[:, j, a:a + n])] for j in range(KC) for a, n in COLS]
        under = [[(ks[:, j, :], q[:, j, a:a + n])] for j in range(KC) for a, n in COLS]
        products(g, "a_under", under,
                 lambda e, n, bank: e.tensor_scalar(inv[:, where(n)[0], where(n)[1]], bank, 1e-6, None, ALU.add))
        on_vector(g, [lambda dve: dve.reciprocal(inv[:, :, :], inv[:, :, :])])
        products(g, "a_over", over,
                 lambda e, n, bank: e.tensor_tensor(o[:, where(n)[0], where(n)[1]], bank,
                                                    inv[:, where(n)[0], where(n)[1]], ALU.mult))

        def add_o(dve, n, bank):
            m, cs = where(n)
            return dve.scalar_tensor_tensor(x[:, m, cs], bank, bo[:, m:m + 1], x[:, m, cs], ALU.add, ALU.add)
        products(g, "a_wo_gemm", linear(wo, o), add_o)

    with ExitStack() as s0:
        y = s0.enter_context(nc.sbuf_tensor("e_y", [P, KC, NP], F32))
        layer_norm(g, "ln2", x, xn)
        g.end_phase()
        experts(g, d, 0, 4, xn, y)
        experts(g, d, 1, 8, y, xn)
        on_vector(g, [lambda dve: dve.tensor_tensor(x[:, :, :], x[:, :, :], xn[:, :, :], ALU.add)])


def experts(g, d, level, n_e, src, dst):
    nc = g.nc
    F = 256 // P
    with ExitStack() as s0:
        def sb(name, shape, dt=F32):
            return s0.enter_context(nc.sbuf_tensor(f"e{level}_{name}", shape, dt))

        wr, w1, w2 = sb("wr", [P, KC, n_e]), sb("w1", [P, n_e, KC, 256]), sb("w2", [P, n_e, F, C])
        b1, b2 = sb("b1", [P, n_e * F]), sb("b2", [n_e, C])
        prob, mask = sb("prob", [P, RT, n_e]), sb("mask", [P, RT, n_e])
        left, eq, prio = sb("left", [P, RT, n_e]), sb("eq", [P, RT, n_e]), sb("prio", [P, n_e])
        one = sb("one", [P, RT])
        prob_t, mask_t = sb("prob_t", [n_e, NP]), sb("mask_t", [n_e, NP])
        transfer(g, f"e{level}_in", [
            (wr[:, :, :].rearrange("p k n -> p (k n)"), d[f"e_Wr{level}"]),
            (w1[:, :, :, :].rearrange("p e k n -> p (e k n)"), d[f"e_W1_{level}"]),
            (w2[:, :, :, :].rearrange("p e k n -> p (e k n)"), d[f"e_W2_{level}"]),
            (b1[:, :], d[f"e_b1_{level}"]), (b2[:, :], d[f"e_b2_{level}"])])
        products(g, f"e{level}_router", rows_of(wr, src),
                 lambda e, n, bank: e.tensor_copy(prob[:, n, :], bank))
        wide = lambda ap: ap.unsqueeze(2).broadcast_to([P, RT, n_e])
        on_vector(g, [
            lambda dve: dve.tensor_reduce(one[:, :], prob[:, :, :], AX.X, ALU.max),
            lambda dve: dve.tensor_tensor(prob[:, :, :], prob[:, :, :], wide(one[:, :]), ALU.subtract)])
        on_scalar(g, f"e{level}_exp", [lambda act: act.activation(prob[:, :, :], prob[:, :, :], ACT.Exp)])

        def greatest(first):
            return [
                lambda dve: dve.tensor_reduce(one[:, :], left[:, :, :], AX.X, ALU.max),
                lambda dve: dve.tensor_tensor(eq[:, :, :], left[:, :, :], wide(one[:, :]), ALU.is_equal),
                lambda dve: dve.tensor_tensor(eq[:, :, :], eq[:, :, :],
                                              prio[:, :].unsqueeze(1).broadcast_to([P, RT, n_e]), ALU.mult),
                lambda dve: dve.tensor_reduce(one[:, :], eq[:, :, :], AX.X, ALU.max),
                lambda dve: dve.tensor_tensor(eq[:, :, :], eq[:, :, :], wide(one[:, :]), ALU.is_equal),
                lambda dve: dve.scalar_tensor_tensor(left[:, :, :], eq[:, :, :], -2.0, left[:, :, :],
                                                     ALU.mult, ALU.add),
                (lambda dve: dve.tensor_copy(mask[:, :, :], eq[:, :, :])) if first else
                (lambda dve: dve.tensor_tensor(mask[:, :, :], mask[:, :, :], eq[:, :, :], ALU.add))]
        on_vector(g, [
            lambda dve: dve.tensor_reduce(one[:, :], prob[:, :, :], AX.X, ALU.add),
            lambda dve: dve.reciprocal(one[:, :], one[:, :]),
            lambda dve: dve.tensor_tensor(prob[:, :, :], prob[:, :, :], wide(one[:, :]), ALU.mult),
            lambda dve: dve.tensor_copy(left[:, :, :], prob[:, :, :]),
            lambda dve: dve.tensor_scalar(prio[:, :], g.numbers_f[:, 0:n_e], -1.0, float(n_e), ALU.mult, ALU.add),
        ] + greatest(True) + greatest(False))
        for name, rows, cols in (("p", prob, prob_t), ("m", mask, mask_t)):
            transposes(g, f"e{level}_turn_{name}", [rows[:, i, :] for i in range(RT)],
                       lambda j, n, cols=cols: cols[:, j * 4 * P:(j * 4 + n) * P].rearrange("e (n m) -> e n m", m=P))

        turns = [(a, w, e) for a, w in COLS for e in range(n_e)]
        p_all, m_all = sb("p_all", [P, 2, 512]), sb("m_all", [P, 2, 512])
        masked, hid = sb("masked", [P, 2, F, 512]), sb("hid", [P, 2, F, 512])
        y_bank = [s0.enter_context(nc.psum_tensor(f"e{level}_y{m}", [P, 512], F32)) for m in range(KC)]
        h_bank = [s0.enter_context(nc.psum_tensor(f"e{level}_h{f}", [P, 512], F32)) for f in range(F)]
        spread = [s0.enter_context(nc.psum_tensor(f"e{level}_s{i}", [P, 512], F32)) for i in range(2)]
        sem = {n: s0.enter_context(g.semaphore(f"e{level}_{n}")) for n in
               ("spread", "copied", "hidden", "masked", "relu", "weighed", "summed", "stored")}
        block = s0.enter_context(nc.Block(no_gpsimd_drain=True))

        @block.tensor
        def _(pe):
            def first_layer(n):
                a, w, e = turns[n]
                if n >= 1:
                    pe.wait_ge(sem["copied"], n)
                pe.matmul(spread[0][:, 0:w], g.sel[0:n_e, e, :], prob_t[:, a:a + w], start=True, stop=True)
                pe.matmul(spread[1][:, 0:w], g.sel[0:n_e, e, :], mask_t[:, a:a + w], start=True,
                          stop=True).then_inc(sem["spread"], 1)
                if n >= 1:
                    pe.wait_ge(sem["masked"], n)
                for f in range(F):
                    for k in range(KC):
                        mm = pe.matmul(h_bank[f][:, 0:w], w1[:, e, k, f * P:(f + 1) * P], src[:, k, a:a + w],
                                       start=(k == 0), stop=(k == KC - 1))
                mm.then_inc(sem["hidden"], 1)

            def second_layer(n):
                a, w, e = turns[n]
                if e == 0 and n > 0:
                    pe.wait_ge(sem["stored"], n // n_e)
                if e == 0:
                    for m in range(KC):
                        pe.matmul(y_bank[m][:, 0:w], b2[:, m * P:(m + 1) * P], prob_t[:, a:a + w], start=True,
                                  stop=False)
                pe.wait_ge(sem["weighed"], n + 1)
                for m in range(KC):
                    for f in range(F):
                        mm = pe.matmul(y_bank[m][:, 0:w], w2[:, e, f, m * P:(m + 1) * P], hid[:, n % 2, f, 0:w],
                                       start=False, stop=(e == n_e - 1 and f == F - 1))
                mm.then_inc(sem["summed"], 1)
            first_layer(0)
            for n in range(len(turns)):
                if n + 1 < len(turns):
                    first_layer(n + 1)
                second_layer(n)

        @block.scalar
        def _(act):
            for n, (a, w, e) in enumerate(turns):
                act.wait_ge(sem["spread"], n + 1)
                if n >= 2:
                    act.wait_ge(sem["weighed"], n - 1)
                act.activation(p_all[:, n % 2, 0:w], spread[0][:, 0:w], ACT.Copy)
                act.activation(m_all[:, n % 2, 0:w], spread[1][:, 0:w], ACT.Copy).then_inc(sem["copied"], 1)
                act.wait_ge(sem["masked"], n + 1)
                for f in range(F):
                    ins = act.activation(masked[:, n % 2, f, 0:w], masked[:, n % 2, f, 0:w], ACT.Relu,
                                         bias=b1[:, e * F + f:e * F + f + 1])
                ins.then_inc(sem["relu"], 1)

        @block.vector
        def _(dve):
            for n, (a, w, e) in enumerate(turns):
                dve.wait_ge(sem["copied"], n + 1)
                dve.wait_ge(sem["hidden"], n + 1)
                for f in range(F):
                    ins = dve.tensor_tensor(masked[:, n % 2, f, 0:w], h_bank[f][:, 0:w], m_all[:, n % 2, 0:w],
                                            ALU.mult)
                ins.then_inc(sem["masked"], 1)
                dve.wait_ge(sem["relu"], n + 1)
                if n >= 2:
                    dve.wait_ge(sem["summed"], n - 1)
                for f in range(F):
                    ins = dve.tensor_tensor(hid[:, n % 2, f, 0:w], masked[:, n % 2, f, 0:w],
                                            p_all[:, n % 2, 0:w], ALU.mult)
                ins.then_inc(sem["weighed"], 1)
                if e == n_e - 1:
                    dve.wait_ge(sem["summed"], n + 1)
                    for m in range(KC):
                        ins = dve.tensor_copy(dst[:, m, a:a + w], y_bank[m][:, 0:w])
                    ins.then_inc(sem["stored"], 1)


def kernel(**inputs):
    import concourse.bacc as bacc
    from concourse.bass_utils import run_bass_kernel_spmd

    a = {n: np.asarray(v) for n, v in inputs.items()}

    def weight(w):
        return w.reshape(-1, P, w.shape[-1]).transpose(1, 0, 2).reshape(P, -1)

    def column(b):
        return b.reshape(-1, P).T

    def row(b):
        return b.reshape(1, -1)

    x = np.zeros((NP, C), np.float32)
    x[:N] = a["x"]
    src = np.full(EP, NP - 1, np.int32)
    src[:E] = a["src"]
    dst = np.zeros(EP, np.int32)
    dst[:E] = a["dst"]
    attr = np.zeros((EP, H), np.float32)
    attr[:E] = a["edge_attr_8"]
    L = {"x": weight(x.T), "src": src.reshape(P, ET), "dst": dst.reshape(P, ET),
         "attr": attr.reshape(P, ET * H), "src_by_tile": src.reshape(P, ET).T.reshape(1, -1)}
    for n in "qkv":
        L[f"g_W{n}"] = weight(a[f"L0_gnn_W{n}"].T)
        L[f"g_b{n}"] = row(a[f"L0_gnn_b{n}"])
    L["g_Wo"], L["g_bo"] = weight(a["L0_gnn_Wo"].T), column(a["L0_gnn_bo"])
    L["g_W1"], L["g_b1"] = weight(a["L0_gnn_W1"].T), column(a["L0_gnn_b1"])
    L["g_W2"], L["g_b2"] = weight(a["L0_gnn_W2"].T), column(a["L0_gnn_b2"])
    for n in ("ln_att_g", "ln_att_b", "ln_ff_g", "ln_ff_b"):
        L[n] = column(a[f"L0_gnn_{n}"])
    for n in ("Wq", "Wk", "Wv", "W1", "W2"):
        L[f"m_{n}"] = weight(a[f"L0_mix_{n}"].T)
    order = "fioc"
    L["l_Wx"] = weight(np.concatenate([a[f"L0_ffn_W_{n}"][:C] for n in order], 1))
    L["l_Wh"] = weight(np.stack([a[f"L0_ffn_W_{n}"][C:].reshape(C, KC, P) for n in order], 2).reshape(C, -1))
    L["l_b"] = np.stack([a[f"L0_ffn_b_{n}"].reshape(KC, P) for n in order], 1).reshape(M16, P).T
    L["c_W1"], L["c_b1"] = weight(a["L1_gnn_W1"]), row(a["L1_gnn_b1"])
    L["c_W2"], L["c_b2"] = weight(a["L1_gnn_W2"]), row(a["L1_gnn_b2"])
    for n in "qkvo":
        L[f"a_W{n}"] = weight(a[f"L1_mix_W{n}"].T)
        L[f"a_b{n}"] = (row if n in "kv" else column)(a[f"L1_mix_b{n}"])
    for i in range(2):
        n_e = a[f"L1_ffn_Wr{i}"].shape[1]
        L[f"e_Wr{i}"] = weight(a[f"L1_ffn_Wr{i}"])
        L[f"e_W1_{i}"] = a[f"L1_ffn_W1_{i}"].reshape(n_e * KC, P, 256).transpose(1, 0, 2).reshape(P, -1)
        L[f"e_b1_{i}"] = column(a[f"L1_ffn_b1_{i}"].reshape(-1))
        L[f"e_W2_{i}"] = a[f"L1_ffn_W2_{i}"].reshape(n_e * 2, P, C).transpose(1, 0, 2).reshape(P, -1)
        L[f"e_b2_{i}"] = a[f"L1_ffn_b2_{i}"]

    nc = bacc.Bacc("TRN2", target_bir_lowering=False, num_devices=1)
    d, arrays = {}, {}
    for n, v in L.items():
        v = np.ascontiguousarray(v)
        arrays[f"in_{n}"] = v
        d[n] = nc.dram_tensor(f"in_{n}", v.shape, mybir.dt.from_np(v.dtype), kind="ExternalInput").ap()
    out = nc.dram_tensor("result", (P, KC * NP), F32, kind="ExternalOutput").ap()
    kernel_body(nc, d, out)
    r = run_bass_kernel_spmd(nc, [arrays], core_ids=[0]).results[0]["result"]
    return np.ascontiguousarray(r.reshape(P, KC, NP).transpose(1, 0, 2).reshape(C, NP).T[:N])
```
